# Optimizing a Trainium2 kernel written in Bass

```python
import numpy as np
import jax
import jax.numpy as jnp

def _softmax(x, axis=-1):
    return jax.nn.softmax(x, axis=axis)

def _gelu(x):
    return jax.nn.gelu(x, approximate=True)

def _silu(x):
    return jax.nn.silu(x)

def _sigmoid(x):
    return jax.nn.sigmoid(x)

def _layernorm(x, axis=-1, eps=1e-05):
    m = jnp.mean(x, axis=axis, keepdims=True)
    v = jnp.var(x, axis=axis, keepdims=True)
    return (x - m) / jnp.sqrt(v + eps)

def _scatter_add(tgt, idx, src, axis=0):
    return tgt.at[idx].add(src)

def _segment_sum(src, seg, n):
    return jax.ops.segment_sum(src, seg, n)
kernel_name = 'mk_adaln_d1_jaxref_r8_27b5dc'

def setup_inputs(seed: int=0):
    np.random.seed(seed)
    _w = jnp.asarray

    def _L0_attn_setup():
        import jax, jax.numpy as jnp
        import numpy as np
        from jax import lax
        B, T, D, H, CS = (4, 512, 256, 16, 64)
        DK = D // H

        def apply_rope(x):
            t, d = (x.shape[-2], x.shape[-1])
            inv_freq = 1.0 / 10000.0 ** (jnp.arange(0, d, 2, dtype=jnp.float32) / d)
            pos = jnp.arange(t, dtype=jnp.float32)
            sinusoid = pos[:, None] * inv_freq[None, :]
            sin, cos = (jnp.sin(sinusoid), jnp.cos(sinusoid))
            x1, x2 = (x[..., ::2], x[..., 1::2])
            out = jnp.stack([x1 * cos - x2 * sin, x1 * sin + x2 * cos], axis=-1)
            return out.reshape(x.shape)
        key = jax.random.key(seed)
        ks = jax.random.split(key, 6)
        s = 0.02
        return {'x': jax.random.normal(ks[0], (B, T, D), dtype=jnp.float32), 'Wq': jax.random.normal(ks[1], (D, D), dtype=jnp.float32) * s, 'bq': jnp.zeros((D,), jnp.float32), 'Wk': jax.random.normal(ks[2], (D, D), dtype=jnp.float32) * s, 'bk': jnp.zeros((D,), jnp.float32), 'Wv': jax.random.normal(ks[3], (D, D), dtype=jnp.float32) * s, 'bv': jnp.zeros((D,), jnp.float32), 'Wg': jax.random.normal(ks[4], (D, D), dtype=jnp.float32) * s, 'bg': jnp.zeros((D,), jnp.float32), 'Wo': jax.random.normal(ks[5], (D, D), dtype=jnp.float32) * s, 'bo': jnp.zeros((D,), jnp.float32)}
    _L0_attn_in = _L0_attn_setup()

    def _L0_ffn_setup():
        import jax, jax.numpy as jnp
        import numpy as np
        D_MODEL = 256
        D_EXPERT = 1024
        EPS = 1e-08

        def ternary_quant(w):
            scale = jnp.mean(jnp.abs(w)) + EPS
            q = jnp.clip(jnp.round(w / scale), -1.0, 1.0) * scale
            return w + jax.lax.stop_gradient(q - w)
        key = jax.random.key(seed)
        k_x, k_up, k_gate, k_down = jax.random.split(key, 4)
        std_in = 1.0 / np.sqrt(D_MODEL)
        std_exp = 1.0 / np.sqrt(D_EXPERT)
        return {'x': jax.random.normal(k_x, (4, 256, D_MODEL), dtype=jnp.float32), 'W_up': jax.random.normal(k_up, (D_EXPERT, D_MODEL), dtype=jnp.float32) * std_in, 'W_gate': jax.random.normal(k_gate, (D_EXPERT, D_MODEL), dtype=jnp.float32) * std_in, 'W_down': jax.random.normal(k_down, (D_MODEL, D_EXPERT), dtype=jnp.float32) * std_exp}
    _L0_ffn_in = _L0_ffn_setup()
    _L0_c = _w((lambda *s: np.random.randn(*s).astype(np.float32) * 0.05)(2, 256))
    _L0_wmod = _w((lambda *s: np.random.randn(*s).astype(np.float32) * 0.05)(256, 6 * 256) * 256 ** (-0.5))
    _d = {'L0_attn_x': _L0_attn_in['x'], 'L0_attn_Wq': _L0_attn_in['Wq'], 'L0_attn_bq': _L0_attn_in['bq'], 'L0_attn_Wk': _L0_attn_in['Wk'], 'L0_attn_bk': _L0_attn_in['bk'], 'L0_attn_Wv': _L0_attn_in['Wv'], 'L0_attn_bv': _L0_attn_in['bv'], 'L0_attn_Wg': _L0_attn_in['Wg'], 'L0_attn_bg': _L0_attn_in['bg'], 'L0_attn_Wo': _L0_attn_in['Wo'], 'L0_attn_bo': _L0_attn_in['bo'], 'L0_ffn_W_up': _L0_ffn_in['W_up'], 'L0_ffn_W_gate': _L0_ffn_in['W_gate'], 'L0_ffn_W_down': _L0_ffn_in['W_down'], 'L0_c': _L0_c, 'L0_wmod': _L0_wmod}
    _x0 = _d['L0_attn_x']
    _d['L0_attn_x'] = jax.random.normal(jax.random.fold_in(jax.random.key(seed), 1), (2, 2048, 256), dtype=_x0.dtype)
    del _x0
    return _d

def reference(L0_attn_x, L0_attn_Wq, L0_attn_bq, L0_attn_Wk, L0_attn_bk, L0_attn_Wv, L0_attn_bv, L0_attn_Wg, L0_attn_bg, L0_attn_Wo, L0_attn_bo, L0_ffn_W_up, L0_ffn_W_gate, L0_ffn_W_down, L0_c, L0_wmod):

    def _L0_attn_ref(x, Wq, bq, Wk, bk, Wv, bv, Wg, bg, Wo, bo):
        import jax, jax.numpy as jnp
        import numpy as np
        from jax import lax
        B, T, D, H, CS = (4, 512, 256, 16, 64)
        DK = D // H

        def apply_rope(x):
            t, d = (x.shape[-2], x.shape[-1])
            inv_freq = 1.0 / 10000.0 ** (jnp.arange(0, d, 2, dtype=jnp.float32) / d)
            pos = jnp.arange(t, dtype=jnp.float32)
            sinusoid = pos[:, None] * inv_freq[None, :]
            sin, cos = (jnp.sin(sinusoid), jnp.cos(sinusoid))
            x1, x2 = (x[..., ::2], x[..., 1::2])
            out = jnp.stack([x1 * cos - x2 * sin, x1 * sin + x2 * cos], axis=-1)
            return out.reshape(x.shape)
        b, t, c = x.shape
        h, dk, cs = (H, DK, CS)
        nc = t // cs

        def heads(y):
            return y.reshape(b, t, h, dk).transpose(0, 2, 1, 3)
        q = heads(x @ Wq.T + bq)
        k = heads(x @ Wk.T + bk)
        v = heads(x @ Wv.T + bv)
        g = jax.nn.sigmoid(heads(x @ Wg.T + bg))
        q = jax.nn.elu(apply_rope(q)) + 1.0
        k = jax.nn.elu(apply_rope(k)) + 1.0

        def chunked(y):
            return y.reshape(b, h, nc, cs, dk).transpose(2, 0, 1, 3, 4)
        qc, kc, vc, gc = (chunked(q), chunked(k), chunked(v), chunked(g))
        S0 = jnp.zeros((b, h, dk, dk), x.dtype)
        Z0 = jnp.zeros((b, h, dk), x.dtype)

        def step(carry, inp):
            S, Z = carry
            qi, ki, vi, gi = inp
            S = S + jnp.einsum('bhtd,bhte->bhde', ki, vi)
            Z = Z + ki.sum(axis=2)
            num = jnp.einsum('bhtd,bhde->bhte', qi, S)
            den = jnp.einsum('bhtd,bhd->bht', qi, Z)[..., None] + 1e-06
            return ((S, Z), gi * num / den)
        _, out = lax.scan(step, (S0, Z0), (qc, kc, vc, gc))
        out = out.transpose(1, 2, 0, 3, 4).reshape(b, h, t, dk)
        out = out.transpose(0, 2, 1, 3).reshape(b, t, c)
        return out @ Wo.T + bo

    def _L0_ffn_ref(x, W_up, W_gate, W_down):
        import jax, jax.numpy as jnp
        import numpy as np
        D_MODEL = 256
        D_EXPERT = 1024
        EPS = 1e-08

        def ternary_quant(w):
            scale = jnp.mean(jnp.abs(w)) + EPS
            q = jnp.clip(jnp.round(w / scale), -1.0, 1.0) * scale
            return w + jax.lax.stop_gradient(q - w)
        wu = ternary_quant(W_up)
        wg = ternary_quant(W_gate)
        wd = ternary_quant(W_down)
        up = jnp.einsum('bsd,ed->bse', x, wu)
        gate = jnp.einsum('bsd,ed->bse', x, wg)
        hidden = jax.nn.silu(up) * gate
        return jnp.einsum('bse,de->bsd', hidden, wd)
    x = L0_attn_x
    mod = (_silu(L0_c) @ L0_wmod).reshape(L0_c.shape[0], 6, 1, -1)
    sa, ca, ga, sb, cb, gb = (mod[:, 0], mod[:, 1], mod[:, 2], mod[:, 3], mod[:, 4], mod[:, 5])
    ga = (2 * (ga >= 0) - 1) * jnp.maximum(jnp.abs(ga), 0.25)
    gb = (2 * (gb >= 0) - 1) * jnp.maximum(jnp.abs(gb), 0.25)
    h = _layernorm(x, axis=-1) * (1 + ca) + sa
    x = x + ga * _L0_attn_ref(h, L0_attn_Wq, L0_attn_bq, L0_attn_Wk, L0_attn_bk, L0_attn_Wv, L0_attn_bv, L0_attn_Wg, L0_attn_bg, L0_attn_Wo, L0_attn_bo)
    h = _layernorm(x, axis=-1) * (1 + cb) + sb
    x = x + gb * _L0_ffn_ref(h, L0_ffn_W_up, L0_ffn_W_gate, L0_ffn_W_down)
    return x

_drawn_inputs = setup_inputs


def setup_inputs(seed=0):
    import zlib

    import numpy as np

    out = dict(_drawn_inputs(seed))
    spreads = {'L0_attn_bq': (0.0, 2.0),
     'L0_attn_bk': (0.0, 2.0),
     'L0_attn_bv': (0.0, 0.8),
     'L0_attn_bg': (0.0, 0.8),
     'L0_attn_bo': (0.0, 0.331)}
    factors = {'L0_attn_Wq': 31.701,
     'L0_attn_Wk': 22.681,
     'L0_attn_Wv': 8.0,
     'L0_attn_Wg': 8.0,
     'L0_attn_Wo': 8.0}
    for name, (base, spread) in spreads.items():
        noise = np.random.default_rng([zlib.crc32(name.encode()), seed]).standard_normal(out[name].shape)
        drawn = base * np.exp(spread * noise) if base else spread * noise
        out[name] = jnp.asarray(drawn.astype(out[name].dtype))
    for name, factor in factors.items():
        out[name] = (out[name] * factor).astype(out[name].dtype)
    return out
```

```python
import numpy as np
import concourse.bass as bass
from concourse import mybir
from contextlib import ExitStack

F32 = mybir.dt.float32
F16 = mybir.dt.float16
ALU = mybir.AluOpType
ACT = mybir.ActivationFunctionType

P = 128
B, T, D = 2, 2048, 256
H = 16
DK = D // H
CS = 64
E = 1024
DC = D // P
EC = E // P
TILES = 2
GT = TILES * P
CH = GT // CS
GROUPS = B * T // GT
FIRST = 5
PAIRS = EC // 2
HH = P // DK
VW = P + HH

LN_EPS = 1e-5
Q_EPS = 1e-8
DEN_EPS = 1e-6

S_N = 2.0 ** 5
S_W = 2.0 ** 10
S_O = 2.0 ** 4
S_H = 2.0 ** -7
S_QKVG = S_N * S_W
S_Y = S_O * S_W


def constants():
    inv = np.float32(1.0) / np.power(np.float32(10000.0), np.arange(0, DK, 2, dtype=np.float32) / np.float32(DK))
    ang = np.arange(T, dtype=np.float32)[:, None] * inv[None]
    cos, sin = np.cos(ang), np.sin(ang)
    rope = np.empty((T, 2, DK // 2, 2), np.float32)
    rope[:, 0, :, 0] = cos
    rope[:, 0, :, 1] = cos
    rope[:, 1, :, 0] = -sin
    rope[:, 1, :, 1] = sin
    rope *= np.float32(1.0 / S_QKVG)
    rope = rope.reshape(T // GT, TILES, P, 2 * DK).transpose(0, 2, 1, 3).copy()
    head = np.arange(P) // DK
    mask = np.concatenate([head[:, None] == head[None, :], head[:, None] == np.arange(HH)[None, :]], 1)
    mask = np.stack([mask] * 2, 1).astype(np.float32)
    return rope, mask, np.eye(P, dtype=np.float32)


def block_kernel(nc, x, w_attn, w_out, b_attn, b_out, w_up, w_gate, w_down, c_t, w_mod,
                 rope_t, mask_t, ident_t, out):
    ctx = ExitStack()
    with ctx:
        def sb(name, shape, dt=F32):
            return ctx.enter_context(nc.sbuf_tensor(name, shape, dt))

        def sem(name):
            return ctx.enter_context(nc.semaphore(name))

        ident = sb("ident", [P, P])
        mask = sb("mask", [P, 2, VW])
        c_sb = sb("c_sb", [P, DC, B])
        c_th = sb("c_th", [P, DC, B])
        silu_c = sb("silu_c", [P, DC, B])
        silu_rows = sb("silu_rows", [P, DC, B, P])
        wmod = sb("wmod", [P, DC, 6 * D])
        wa32 = sb("wa32", [P, DC, 4 * D])
        wo32 = sb("wo32", [P, DC, D])
        wf32 = sb("wf32", [P, 3, DC * E])
        ba = sb("ba", [1, 4 * D])
        bo_rows = sb("bo_rows", [P, D])
        ones = sb("ones", [1, P])
        mean_mat = sb("mean_mat", [P, P])
        shift = sb("shift", [P, DC, B, 4])
        sa_rows = sb("sa_rows", [P, DC, P])
        ca_scale = sb("ca_scale", [P, DC, B])
        cb_scale = sb("cb_scale", [P, DC, B])
        sb_shift = sb("sb_shift", [P, DC, B])
        gates = sb("gates", [P, B, 2, D])
        gb_scaled = sb("gb_scaled", [P, B, D])
        bo_scaled = sb("bo_scaled", [P, D])
        wa_hi = sb("wa_hi", [P, B, DC, 4 * D], F16)
        wa_lo = sb("wa_lo", [P, B, DC, 4 * D], F16)
        wo_hi = sb("wo_hi", [P, B, DC, D], F16)
        wo_lo = sb("wo_lo", [P, B, DC, D], F16)
        bias_a = sb("bias_a", [P, 4 * D], F16)
        bias_o = sb("bias_o", [P, D], F16)
        pick_a = sb("pick_a", [P, B, P], F16)
        pick_o = sb("pick_o", [P, B, P], F16)
        abs_sums = sb("abs_sums", [P, 3, 4])
        scale3 = sb("scale3", [P, 3])
        thr = sb("thr", [P, 2, 3])
        tanh_scale = sb("tanh_scale", [P, 1])
        prod3 = sb("prod3", [P, 2])
        below = sb("below", [P, DC * E], F16)
        w3 = sb("w3", [P, 3, DC * E], F16)
        w_up3 = w3[:, 0, :].rearrange("p (c e) -> p c e", c=DC)
        w_gate3 = w3[:, 1, :].rearrange("p (c e) -> p c e", c=DC)
        w_down3 = w3[:, 2, :].rearrange("p (e d) -> p e d", e=EC)
        minus_half = sb("minus_half", [P, TILES])

        x_in = sb("x_in", [P, 2, TILES, D])
        x_res = sb("x_res", [P, 2, TILES, D])
        rope = sb("rope", [P, 2, TILES, 2 * DK])
        stats = sb("stats", [P, 2, TILES, 6])
        mv = sb("mv", [P, 2, TILES, 2])
        var_s = sb("var_s", [P, 2, TILES])
        rstd = sb("rstd", [P, 2, TILES])
        n1 = sb("n1", [P, TILES, D])
        n1_hi = sb("n1_hi", [P, DC, GT], F16)
        n1_lo = sb("n1_lo", [P, DC, GT], F16)
        rot = sb("rot", [P, TILES, 2 * D])
        neg = sb("neg", [P, TILES, 2 * D])
        qk = sb("qk", [P, 2, TILES, 2 * D])
        v_ext = sb("v_ext", [P, 2, TILES, 2, VW])
        gate_t = sb("gate_t", [P, 2, TILES, D])
        q_t = sb("q_t", [P, DC, GT])
        kv_m = sb("kv_m", [P, CH, 2, VW])
        state = sb("state", [P, B, CH, 2, VW])
        den = sb("den", [P, TILES, H])
        rden = sb("rden", [P, TILES, H])
        gated = sb("gated", [P, TILES, D])
        o = sb("o", [P, TILES, D])
        o_hi = sb("o_hi", [P, DC, GT], F16)
        o_lo = sb("o_lo", [P, DC, GT], F16)
        x1 = sb("x1", [P, 2, TILES, D])
        n2 = sb("n2", [P, TILES, D])
        h2 = sb("h2", [P, DC, GT])
        h2_hi = sb("h2_hi", [P, DC, GT], F16)
        h2_lo = sb("h2_lo", [P, DC, GT], F16)
        hid = sb("hid", [P, PAIRS, 2, GT])
        hid_hi = sb("hid_hi", [P, 2, EC, GT], F16)
        hid_lo = sb("hid_lo", [P, 2, EC, GT], F16)
        y2g = sb("y2g", [P, TILES, D])
        out_sb = sb("out_sb", [P, 2, TILES, D])

        gate_sign, gate_abs = hid[:, 0:B], hid[:, B:2 * B]
        wo_scaled = x1[:, 0]
        abs_junk = gated[:].rearrange("p s d -> p (s d)")

        bank = [ctx.enter_context(nc.psum_tensor(f"bank{i}", [P, 512], F32)) for i in range(8)]
        ps_up = [bank[0][:, :].rearrange("p (e t) -> p e t", e=2), bank[2][:, :].rearrange("p (e t) -> p e t", e=2)]
        ps_gate = [bank[1][:, :].rearrange("p (e t) -> p e t", e=2), bank[3][:, :].rearrange("p (e t) -> p e t", e=2)]
        ps_tr = bank[4][:, :].rearrange("p (c t) -> p c t", c=DC)
        ps_qk = bank[5]
        ps_vg = bank[6]
        ps_kv = bank[7][:, 0:2 * VW].rearrange("p (h v) -> p h v", h=2)
        ps_num = [bank[7][:, 0:2 * VW].rearrange("p (h v) -> p h v", h=2),
                  bank[5][:, 0:2 * VW].rearrange("p (h v) -> p h v", h=2)]
        ps_y = bank[5][:, :].rearrange("p (s d) -> p s d", s=TILES)
        ps_y2 = bank[6][:, :].rearrange("p (s d) -> p s d", s=TILES)

        s_small, s_wmod, s_wa, s_wo, s_wf = [sem(f"{n}_loaded") for n in ("small", "wmod", "w_attn", "w_out", "w_ffn")]
        x_loaded = [sem(f"x_loaded{i}") for i in range(2)]
        xr_loaded = [sem(f"xr_loaded{i}") for i in range(2)]
        rope_loaded = [sem(f"rope_loaded{i}") for i in range(2)]
        stored = [sem(f"stored{i}") for i in range(2)]
        c_tanh, silu_made, silu_rows_made = sem("c_tanh"), sem("silu_made"), sem("silu_rows_made")
        mod_cols, mod_rows, shift_made, sa_made = sem("mod_cols"), sem("mod_rows"), sem("shift_made"), sem("sa_made")
        scales_made, gates_part, gates_made = sem("scales_made"), sem("gates_part"), sem("gates_made")
        bias_sum, bias_hi, bias_lo = sem("bias_sum"), sem("bias_hi"), sem("bias_lo")
        wa_hi_made, wa_lo_made, wo_scl, wo_hi_made, wo_lo_made = [
            sem(n) for n in ("wa_hi_made", "wa_lo_made", "wo_scl", "wo_hi_made", "wo_lo_made")]
        bo_scl, bo_hi_made, bo_lo_made = sem("bo_scl"), sem("bo_hi_made"), sem("bo_lo_made")
        abs_made, abs_added, scale_sum, scale_made, thr_made = [
            sem(n) for n in ("abs_made", "abs_added", "scale_sum", "scale_made", "thr_made")]
        below_made, ternary_made, gb_made = sem("below_made"), sem("ternary_made"), sem("gb_made")
        const_made = sem("const_made")
        picks_zeroed, picks_made = sem("picks_zeroed"), sem("picks_made")
        ln_stats = [sem(f"ln{i}_stats") for i in (1, 2)]
        ln_mv = [sem(f"ln{i}_mean_var") for i in (1, 2)]
        ln_var = [sem(f"ln{i}_var_scaled") for i in (1, 2)]
        ln_rstd = [sem(f"ln{i}_rstd") for i in (1, 2)]
        ln_done = [sem(f"ln{i}_normalised") for i in (1, 2)]
        n1_turned, n1_hi_made, n1_lo_made = sem("n1_turned"), sem("n1_hi_made"), sem("n1_lo_made")
        qk_projected, vg_projected = sem("qk_projected"), sem("vg_projected")
        rope_multiplied, rope_added, neg_made, exp_made, qk_made = [
            sem(n) for n in ("rope_multiplied", "rope_added", "neg_made", "exp_made", "qk_made")]
        v_copied, gate_made = sem("v_copied"), sem("gate_made")
        q_turned, q_copied = sem("q_turned"), sem("q_copied")
        kv_summed, kv_masked, state_made = sem("kv_summed"), sem("kv_masked"), sem("state_made")
        num_made, den_made, rden_made, num_gated, o_made = [
            sem(n) for n in ("num_made", "den_made", "rden_made", "num_gated", "o_made")]
        o_turned, o_hi_made, o_lo_made = sem("o_turned"), sem("o_hi_made"), sem("o_lo_made")
        y_made, x1_made = sem("y_made"), sem("x1_made")
        n2_turned, h2_made, h2_hi_made, h2_lo_made = [sem(n) for n in ("n2_turned", "h2_made", "h2_hi_made", "h2_lo_made")]
        up_made, gate_up_made, tanh_made, hid_part, hid_made, hid_hi_made, hid_lo_made = [
            sem(n) for n in ("up_made", "gate_up_made", "tanh_made", "hid_part", "hid_made", "hid_hi_made", "hid_lo_made")]
        y2_made, y2_gated, out_made = sem("y2_made"), sem("y2_gated"), sem("out_made")

        block = ctx.enter_context(nc.Block())

        x_v = x.rearrange("b (g s p) d -> b g p s d", s=TILES, p=P)
        out_v = out.rearrange("b (g s p) d -> b g p s d", s=TILES, p=P)

        def need(eng, semaphore, value):
            if not isinstance(value, int) or value > 0:
                eng.wait_ge(semaphore, value)

        def on(i, g):
            return not isinstance(i, int) or 0 <= g < GROUPS

        def upto(i, g):
            return 2 * i + g + 1 if not isinstance(i, int) else max(0, min(g + 1, GROUPS))

        def steps(eng, step, between=None):
            for t in range(-1, FIRST):
                step(0, t)
                if between:
                    between(t)
            with eng.Fori(0, (GROUPS - 1 - FIRST) // 2) as i:
                step(i, FIRST)
                step(i, FIRST + 1)
            for t in range(GROUPS - 1, GROUPS + 3):
                step(0, t)

        @block.sync
        def _(sp):
            def load_x(i, g):
                need(sp, ln_done[0], TILES * upto(i, g - 2))
                sp.dma_start(x_in[:, g % 2], x_v[g % 2, i + g // 2]).then_inc(x_loaded[g % 2], 16)

            def load_rope(i, g):
                need(sp, rope_multiplied, TILES * upto(i, g - 2))
                sp.dma_start(rope[:, g % 2], rope_t[i + g // 2].rearrange("p (s c) -> p s c", s=TILES))\
                  .then_inc(rope_loaded[g % 2], 16)

            sp.dma_start(c_sb[:], c_t.rearrange("(k p) b -> p k b", p=P)).then_inc(s_small, 16)
            sp.dma_start(ident[:], ident_t).then_inc(s_small, 16)
            sp.dma_start(ba[:], b_attn).then_inc(s_small, 16)
            sp.dma_start(mask[:], mask_t).then_inc(s_small, 16)
            sp.dma_start(wmod[:], w_mod.rearrange("(k p) n -> p k n", p=P)).then_inc(s_wmod, 16)
            load_x(0, 0)
            sp.dma_start(wa32[:], w_attn.rearrange("(c p) n -> p c n", p=P)).then_inc(s_wa, 16)
            load_rope(0, 0)
            load_x(0, 1)
            sp.dma_start(wo32[:], w_out.rearrange("(c p) n -> p c n", p=P)).then_inc(s_wo, 16)
            sp.dma_start(bo_rows[:], b_out.broadcast_to([P, D])).then_inc(s_wo, 16)
            sp.dma_start(wf32[:, 0].rearrange("p (c e) -> p c e", c=DC), w_up.rearrange("(c p) e -> p c e", p=P)).then_inc(s_wf, 16)
            sp.dma_start(wf32[:, 1].rearrange("p (c e) -> p c e", c=DC), w_gate.rearrange("(c p) e -> p c e", p=P)).then_inc(s_wf, 16)
            sp.dma_start(wf32[:, 2].rearrange("p (e d) -> p e d", e=EC), w_down.rearrange("(e p) d -> p e d", p=P)).then_inc(s_wf, 16)

            def step(i, k):
                if on(i, k + 1) and k >= 1:
                    load_x(i, k + 1)
                if on(i, k + 1) and k >= 0:
                    load_rope(i, k + 1)
                if on(i, k):
                    need(sp, x1_made, upto(i, k - 2))
                    sp.dma_start(x_res[:, k % 2], x_v[k % 2, i + k // 2]).then_inc(xr_loaded[k % 2], 16)
                if on(i, k - 3):
                    d = k - 3
                    sp.wait_ge(out_made, upto(i, d))
                    sp.dma_start(out_v[d % 2, i + d // 2], out_sb[:, d % 2]).then_inc(stored[d % 2], 16)

            steps(sp, step)
            for p in range(2):
                sp.wait_ge(stored[p], 16 * (GROUPS // 2))

        @block.gpsimd
        def _(pool):
            nc.gpsimd.memset(ones[:], 1.0).then_inc(const_made, 1)
            nc.gpsimd.memset(mean_mat[:], 1.0 / (D * E)).then_inc(const_made, 1)
            nc.gpsimd.memset(minus_half[:], -0.5).then_inc(const_made, 1)
            nc.gpsimd.memset(pick_a[:], 0.0).then_inc(picks_zeroed, 1)
            nc.gpsimd.memset(pick_o[:], 0.0).then_inc(picks_zeroed, 1)
            nc.gpsimd.memset(state[:, :, CH - 1], 0.0).then_inc(const_made, 1)
            nc.gpsimd.memset(v_ext[:, :, :, :, P:VW], 1.0).then_inc(const_made, 1)
            pool.wait_ge(picks_zeroed, 2)
            pool.wait_ge(const_made, 5)
            n = 0
            for b in range(B):
                for row in (64 * b, 64 * b + 32):
                    for pick, value in ((pick_a, S_N), (pick_o, S_O)):
                        need(pool, picks_made, n)
                        nc.gpsimd.memset(pick[row:row + 1, b, :], value).then_inc(picks_made, 1)
                        n += 1
            pool.wait_ge(picks_made, n)

            def inverse_std(i, g, which):
                pool.wait_ge(ln_var[which], upto(i, g))
                nc.gpsimd.tensor_tensor(rstd[:, which], var_s[:, which], minus_half[:], ALU.pow)\
                  .then_inc(ln_rstd[which], 1)

            def step(i, k):
                nxt, pr, at, ff, dn = k + 1, k, k - 1, k - 2, k - 3

                def add_state(c):
                    pool.wait_ge(kv_masked, CH * (upto(i, at) - 1) + c + 1)
                    nc.gpsimd.tensor_tensor(state[:, at % 2, c], state[:, at % 2, CH - 1], kv_m[:, c], ALU.add)\
                      .then_inc(state_made, 1)

                def add_rope(s):
                    pool.wait_ge(rope_multiplied, TILES * (upto(i, pr) - 1) + s + 1)
                    nc.gpsimd.tensor_tensor(rot[:, s], rot[:, s], neg[:, s], ALU.add).then_inc(rope_added, 1)

                def split_hidden(f, p):
                    pool.wait_ge(hid_hi_made, PAIRS * (upto(i, f) - 1) + p + 1)
                    nc.gpsimd.tensor_tensor(hid_lo[:, f % 2, 2 * p:2 * p + 2], hid[:, p],
                                            hid_hi[:, f % 2, 2 * p:2 * p + 2], ALU.subtract).then_inc(hid_lo_made, 1)

                def divide(s):
                    pool.wait_ge(num_gated, TILES * (upto(i, at) - 1) + s + 1)
                    nc.gpsimd.tensor_tensor(o[:, s].rearrange("p (h e) -> p h e", h=H),
                                            gated[:, s].rearrange("p (h e) -> p h e", h=H),
                                            rden[:, s].unsqueeze(2).broadcast_to([P, H, DK]), ALU.mult)\
                      .then_inc(o_made, 1)

                if on(i, at):
                    add_state(0)
                if on(i, dn):
                    split_hidden(dn, PAIRS - 1)
                if on(i, pr):
                    add_rope(0)
                if on(i, at):
                    add_state(1)
                    add_state(2)
                    add_state(3)
                if on(i, pr):
                    add_rope(1)
                if on(i, nxt):
                    inverse_std(i, nxt, 0)
                if on(i, dn):
                    pool.wait_ge(y2_gated, upto(i, dn))
                    need(pool, stored[dn % 2], 16 * (i + dn // 2))
                    nc.gpsimd.tensor_tensor(out_sb[:, dn % 2], y2g[:], x1[:, dn % 2], ALU.add).then_inc(out_made, 1)
                if on(i, at):
                    divide(0)
                    divide(1)
                if on(i, ff):
                    split_hidden(ff, 0)
                    split_hidden(ff, 1)
                    split_hidden(ff, 2)
                if on(i, at):
                    inverse_std(i, at, 1)

            steps(pool, step)

        @block.scalar
        def _(act):
            act.wait_ge(s_small, 4 * 16)
            nc.scalar.activation(c_th[:], c_sb[:], ACT.Tanh, scale=0.5).then_inc(c_tanh, 1)
            act.wait_ge(scales_made, 1)
            act.wait_ge(s_wa, 16)
            for b in range(B):
                for c in range(DC):
                    nc.scalar.activation(wa_hi[:, b, c], wa32[:, c], ACT.Copy, scale=ca_scale[:, c, b:b + 1])\
                      .then_inc(wa_hi_made, 1)
            act.wait_ge(bias_sum, 2)
            for half in range(2):
                nc.scalar.activation(bias_a[:, 512 * half:512 * (half + 1)], bank[half][:], ACT.Copy, scale=S_W)\
                  .then_inc(bias_hi, 1)

            def setup(t):
                if t == -1:
                    for b in range(B):
                        act.wait_ge(wo_scl, b + 1)
                        nc.scalar.activation(wo_hi[:, b], wo_scaled, ACT.Copy).then_inc(wo_hi_made, 1)
                    act.wait_ge(bo_scl, 2)
                    nc.scalar.activation(bias_o[:], bo_scaled[:], ACT.Copy).then_inc(bo_hi_made, 1)
                    act.wait_ge(s_wf, 3 * 16)
                    for m in range(3):
                        for q in range(4):
                            n = 4 * m + q
                            need(act, abs_made, n)
                            nc.scalar.activation(abs_junk, wf32[:, m, 512 * q:512 * (q + 1)], ACT.Abs,
                                                 accum_out=abs_sums[:, m, q:q + 1]).then_inc(abs_made, 1)

            def step(i, k):
                nxt, pr, at, ff, dn = k + 1, k, k - 1, k - 2, k - 3

                def keys_exp(s):
                    act.wait_ge(neg_made, TILES * (upto(i, pr) - 1) + s + 1)
                    nc.scalar.activation(neg[:, s], neg[:, s], ACT.Exp).then_inc(exp_made, 1)

                def values_and_gate(s):
                    n = TILES * (upto(i, pr) - 1) + s + 1
                    act.wait_ge(vg_projected, n)
                    nc.scalar.activation(v_ext[:, pr % 2, s, :, 0:P],
                                         ps_vg[:, 0:D].rearrange("p (h v) -> p h v", h=2), ACT.Copy,
                                         scale=S_O / S_QKVG).then_inc(v_copied, 1)
                    nc.scalar.activation(gate_t[:, pr % 2, s], ps_vg[:, D:2 * D], ACT.Tanh,
                                         scale=0.5 / S_QKVG).then_inc(gate_made, 1)

                def tanh_up(p):
                    n = PAIRS * (upto(i, ff) - 1) + p + 1
                    act.wait_ge(up_made, n)
                    need(act, hid_lo_made, n - PAIRS)
                    nc.scalar.activation(hid[:, p], ps_up[p % 2], ACT.Tanh, scale=tanh_scale[:, 0:1])\
                      .then_inc(tanh_made, 1)

                def hidden_high(f, p):
                    act.wait_ge(hid_made, PAIRS * (upto(i, f) - 1) + p + 1)
                    nc.scalar.activation(hid_hi[:, f % 2, 2 * p:2 * p + 2], hid[:, p], ACT.Copy)\
                      .then_inc(hid_hi_made, 1)

                if on(i, at):
                    act.wait_ge(q_turned, upto(i, at))
                    nc.scalar.activation(q_t[:], ps_tr, ACT.Copy).then_inc(q_copied, 1)
                if on(i, dn):
                    hidden_high(dn, PAIRS - 1)
                if on(i, pr):
                    keys_exp(0)
                if on(i, ff):
                    act.wait_ge(n2_turned, upto(i, ff))
                    for c in range(DC):
                        nc.scalar.activation(h2[:, c], ps_tr[:, c], ACT.Identity,
                                             scale=cb_scale[:, c, ff % 2:ff % 2 + 1],
                                             bias=sb_shift[:, c, ff % 2:ff % 2 + 1]).then_inc(h2_made, 1)
                    act.wait_ge(h2_made, DC * upto(i, ff))
                    nc.scalar.activation(h2_hi[:], h2[:], ACT.Copy).then_inc(h2_hi_made, 1)
                if on(i, pr):
                    keys_exp(1)
                if on(i, ff):
                    tanh_up(0)
                if on(i, pr):
                    values_and_gate(0)
                if on(i, ff):
                    hidden_high(ff, 0)
                    tanh_up(1)
                if on(i, at):
                    act.wait_ge(o_turned, upto(i, at))
                    nc.scalar.activation(o_hi[:], ps_tr, ACT.Copy).then_inc(o_hi_made, 1)
                if on(i, ff):
                    hidden_high(ff, 1)
                if on(i, pr):
                    values_and_gate(1)
                if on(i, ff):
                    tanh_up(2)
                    hidden_high(ff, 2)
                if on(i, nxt):
                    act.wait_ge(n1_turned, upto(i, nxt))
                    nc.scalar.activation(n1_hi[:], ps_tr, ACT.Copy).then_inc(n1_hi_made, 1)
                if on(i, ff):
                    tanh_up(3)

            steps(act, step, setup)

        @block.vector
        def _(dve):
            dve.wait_ge(c_tanh, 1)
            nc.vector.scalar_tensor_tensor(silu_c[:], c_th[:], 1.0, c_sb[:], ALU.add, ALU.mult).then_inc(silu_made, 1)
            dve.wait_ge(silu_made, 1)
            nc.vector.tensor_scalar(silu_rows[:].rearrange("p c b n -> p (c b) n"),
                                    silu_c[:].rearrange("p c b -> p (c b)").unsqueeze(2).broadcast_to([P, DC * B, P]),
                                    0.5, None, ALU.mult).then_inc(silu_rows_made, 1)
            dve.wait_ge(mod_cols, 1)
            nc.vector.tensor_scalar(shift[:], bank[4][:, 0:DC * B * 4].rearrange("p (c b n) -> p c b n", c=DC, b=B),
                                    0.5, None, ALU.mult).then_inc(shift_made, 1)
            dve.wait_ge(shift_made, 1)
            nc.vector.tensor_scalar(ca_scale[:], shift[:, :, :, 1], 1.0, S_W, ALU.add, ALU.mult).then_inc(scales_made, 1)
            nc.vector.tensor_scalar(cb_scale[:], shift[:, :, :, 3], 1.0, None, ALU.add).then_inc(scales_made, 1)
            nc.vector.tensor_scalar(sb_shift[:], shift[:, :, :, 2], S_N, None, ALU.mult).then_inc(scales_made, 1)
            for b in range(B):
                nc.vector.tensor_copy(sa_rows[:, :, 64 * b:64 * (b + 1)],
                                      shift[:, :, b, 0:1].broadcast_to([P, DC, 64])).then_inc(sa_made, 1)
            dve.wait_ge(scales_made, 3)
            dve.wait_ge(s_wa, 16)
            for b in range(B):
                for c in range(DC):
                    dve.wait_ge(wa_hi_made, DC * b + c + 1)
                    nc.vector.scalar_tensor_tensor(wa_lo[:, b, c], wa32[:, c], ca_scale[:, c, b:b + 1], wa_hi[:, b, c],
                                                   ALU.mult, ALU.subtract).then_inc(wa_lo_made, 1)
            for half in range(2):
                dve.wait_ge(bias_hi, half + 1)
                for b in range(B):
                    r = slice(64 * b + 32, 64 * b + 64)
                    cols = slice(512 * half, 512 * (half + 1))
                    nc.vector.scalar_tensor_tensor(bias_a[r, cols], bank[half][r, :], S_W, bias_a[r, cols],
                                                   ALU.mult, ALU.subtract).then_inc(bias_lo, 1)

            def setup(t):
                if t == -1:
                    dve.wait_ge(mod_rows, 2)
                    for b in range(B):
                        rows = bank[2 + b][:, :].rearrange("p (k d) -> p k d", k=2)
                        nc.vector.tensor_scalar(gate_sign[:, b], rows, 0.0, 2.0, ALU.is_ge, ALU.mult).then_inc(gates_part, 1)
                        dve.wait_ge(gates_part, 2 * b + 1)
                        nc.vector.scalar_tensor_tensor(gate_abs[:, b], gate_sign[:, b], 1.0, rows, ALU.subtract, ALU.mult)\
                          .then_inc(gates_part, 1)
                    dve.wait_ge(gates_part, 4)
                    nc.vector.tensor_scalar(gate_sign, gate_sign, 1.0, None, ALU.subtract).then_inc(gates_part, 1)
                    dve.wait_ge(gates_part, 5)
                    nc.vector.scalar_tensor_tensor(gates[:], gate_abs, 0.25, gate_sign, ALU.max, ALU.mult).then_inc(gates_made, 1)
                    dve.wait_ge(gates_made, 1)
                    dve.wait_ge(s_wo, 32)
                    for b in range(B):
                        need(dve, wo_lo_made, b)
                        nc.vector.scalar_tensor_tensor(wo_scaled, wo32[:], 0.5 * S_W,
                                                       gates[:, b, 0:1].broadcast_to([P, DC, D]),
                                                       ALU.mult, ALU.mult).then_inc(wo_scl, 1)
                        dve.wait_ge(wo_hi_made, b + 1)
                        nc.vector.tensor_tensor(wo_lo[:, b], wo_scaled, wo_hi[:, b], ALU.subtract).then_inc(wo_lo_made, 1)
                    for b in range(B):
                        r = slice(64 * b, 64 * b + 64)
                        nc.vector.scalar_tensor_tensor(bo_scaled[r], bo_rows[r], S_W, gates[r, b, 0],
                                                       ALU.mult, ALU.mult).then_inc(bo_scl, 1)
                    dve.wait_ge(bo_hi_made, 1)
                    for b in range(B):
                        r = slice(64 * b + 32, 64 * b + 64)
                        nc.vector.tensor_tensor(bias_o[r], bo_scaled[r], bias_o[r], ALU.subtract).then_inc(bo_lo_made, 1)
                if t == 0:
                    dve.wait_ge(abs_made, 12)
                    nc.vector.tensor_reduce(scale3[:], abs_sums[:], axis=mybir.AxisListType.X, op=ALU.add).then_inc(abs_added, 1)
                    dve.wait_ge(scale_sum, 1)
                    nc.vector.tensor_scalar(scale3[:], bank[0][:, 0:3], Q_EPS, None, ALU.add).then_inc(scale_made, 1)
                    dve.wait_ge(scale_made, 1)
                    nc.vector.tensor_scalar(thr[:, 0], scale3[:], 0.5, None, ALU.mult).then_inc(thr_made, 1)
                    nc.vector.tensor_scalar(thr[:, 1], scale3[:], -0.5, None, ALU.mult).then_inc(thr_made, 1)
                    nc.vector.tensor_scalar(tanh_scale[:], scale3[:, 0:1], 0.5 / S_N, None, ALU.mult).then_inc(thr_made, 1)
                    nc.vector.tensor_tensor(prod3[:, 0:1], scale3[:, 0:1], scale3[:, 1:2], ALU.mult).then_inc(thr_made, 1)
                    dve.wait_ge(thr_made, 4)
                    nc.vector.tensor_tensor(prod3[:, 1:2], prod3[:, 0:1], scale3[:, 2:3], ALU.mult).then_inc(thr_made, 1)
                    dve.wait_ge(thr_made, 5)
                    nc.vector.tensor_scalar(gb_scaled[:], gates[:, :, 1], prod3[:, 1:2], 0.5 / S_H, ALU.mult, ALU.mult)\
                      .then_inc(gb_made, 1)
                    for m in range(3):
                        need(dve, ternary_made, m)
                        nc.vector.tensor_scalar(below[:], wf32[:, m], thr[:, 1, m:m + 1], None, ALU.is_lt).then_inc(below_made, 1)
                        dve.wait_ge(below_made, m + 1)
                        nc.vector.scalar_tensor_tensor(w3[:, m], wf32[:, m], thr[:, 0, m:m + 1], below[:],
                                                       ALU.is_gt, ALU.subtract).then_inc(ternary_made, 1)

            def tile_stats(i, g, which, src):
                for s in range(TILES):
                    nc.vector.bn_stats(stats[:, which, s], src[:, s]).then_inc(ln_stats[which], 1)

            def mean_var(i, g, which):
                for s in range(TILES):
                    nc.vector.bn_aggr(mv[:, which, s], stats[:, which, s]).then_inc(ln_mv[which], 1)
                dve.wait_ge(ln_mv[which], TILES * upto(i, g))
                nc.vector.tensor_scalar(var_s[:, which], mv[:, which, :, 1], LN_EPS, S_N ** -2, ALU.add, ALU.mult)\
                  .then_inc(ln_var[which], 1)

            def normalise(i, g, which, src, dst):
                dve.wait_ge(ln_rstd[which], upto(i, g))
                for s in range(TILES):
                    nc.vector.tensor_scalar(dst[:, s], src[:, s], mv[:, which, s, 0:1], rstd[:, which, s:s + 1],
                                            ALU.subtract, ALU.mult).then_inc(ln_done[which], 1)

            def step(i, k):
                nxt, pr, at, ff, dn = k + 1, k, k - 1, k - 2, k - 3

                def mask_state(c):
                    dve.wait_ge(kv_summed, CH * (upto(i, at) - 1) + c + 1)
                    nc.vector.tensor_tensor(kv_m[:, c], ps_kv, mask[:], ALU.mult).then_inc(kv_masked, 1)

                def rotate(s):
                    dve.wait_ge(qk_projected, TILES * (upto(i, pr) - 1) + s + 1)
                    if s == 0:
                        dve.wait_ge(rope_loaded[pr % 2], 16 * (i + pr // 2 + 1))
                    heads = ps_qk[:, :].rearrange("p (h f) -> p h f", f=DK)
                    pairs = ps_qk[:, :].rearrange("p (h f u) -> p h f u", f=DK // 2, u=2)
                    nc.vector.tensor_tensor(rot[:, s].rearrange("p (h f) -> p h f", f=DK), heads,
                                            rope[:, pr % 2, s, 0:DK].unsqueeze(1).broadcast_to([P, 2 * H, DK]), ALU.mult)
                    nc.vector.tensor_tensor(neg[:, s].rearrange("p (h f u) -> p h f u", f=DK // 2, u=2), pairs[:, :, :, ::-1],
                                            rope[:, pr % 2, s, DK:2 * DK].rearrange("p (f u) -> p f u", u=2).unsqueeze(1)
                                            .broadcast_to([P, 2 * H, DK // 2, 2]), ALU.mult).then_inc(rope_multiplied, 1)

                def negative(s):
                    n = TILES * (upto(i, pr) - 1) + s + 1
                    dve.wait_ge(rope_added, n)
                    nc.vector.tensor_scalar(neg[:, s], rot[:, s], 0.0, None, ALU.min).then_inc(neg_made, 1)

                def elu_one(s):
                    n = TILES * (upto(i, pr) - 1) + s + 1
                    dve.wait_ge(exp_made, n)
                    nc.vector.scalar_tensor_tensor(qk[:, pr % 2, s], rot[:, s], 0.0, neg[:, s], ALU.max, ALU.add)\
                      .then_inc(qk_made, 1)

                def silu_gate(f, p):
                    n = PAIRS * (upto(i, f) - 1) + p + 1
                    dve.wait_ge(gate_up_made, n)
                    dve.wait_ge(tanh_made, n)
                    nc.vector.scalar_tensor_tensor(hid[:, p], hid[:, p], 1.0, ps_gate[p % 2], ALU.add, ALU.mult)\
                      .then_inc(hid_part, 1)
                    dve.wait_ge(hid_part, n)
                    nc.vector.scalar_tensor_tensor(hid[:, p], hid[:, p], S_H / S_N ** 2, ps_up[p % 2], ALU.mult, ALU.mult)\
                      .then_inc(hid_made, 1)

                def gate_num(s):
                    n = TILES * (upto(i, at) - 1) + s + 1
                    dve.wait_ge(num_made, n)
                    nc.vector.tensor_scalar(den[:, s].rearrange("p (h e) -> p h e", h=2), ps_num[s][:, :, P:VW],
                                            DEN_EPS, None, ALU.add).then_inc(den_made, 1)
                    nc.vector.scalar_tensor_tensor(gated[:, s].rearrange("p (h e) -> p h e", h=2),
                                                   gate_t[:, at % 2, s].rearrange("p (h e) -> p h e", h=2), 1.0,
                                                   ps_num[s][:, :, 0:P], ALU.add, ALU.mult)
                    dve.wait_ge(den_made, n)
                    nc.vector.reciprocal(rden[:, s], den[:, s]).then_inc(num_gated, 1)

                if on(i, dn):
                    silu_gate(dn, PAIRS - 1)
                if on(i, at):
                    mask_state(0)
                if on(i, ff):
                    normalise(i, ff, 1, x1[:, ff % 2], n2)
                if on(i, pr):
                    rotate(0)
                if on(i, at):
                    mask_state(1)
                if on(i, pr):
                    negative(0)
                if on(i, at):
                    mask_state(2)
                if on(i, pr):
                    elu_one(0)
                if on(i, nxt):
                    dve.wait_ge(x_loaded[nxt % 2], 16 * (i + nxt // 2 + 1))
                    tile_stats(i, nxt, 0, x_in[:, nxt % 2])
                    dve.wait_ge(ln_stats[0], TILES * upto(i, nxt))
                if on(i, at):
                    mask_state(3)
                if on(i, pr):
                    rotate(1)
                if on(i, nxt):
                    mean_var(i, nxt, 0)
                if on(i, ff):
                    dve.wait_ge(h2_hi_made, upto(i, ff))
                    nc.vector.tensor_tensor(h2_lo[:], h2[:], h2_hi[:], ALU.subtract).then_inc(h2_lo_made, 1)
                if on(i, dn):
                    dve.wait_ge(y2_made, upto(i, dn))
                    need(dve, out_made, upto(i, dn) - 1)
                    nc.vector.tensor_tensor(y2g[:], ps_y2, gb_scaled[:, dn % 2:dn % 2 + 1].broadcast_to([P, TILES, D]),
                                            ALU.mult).then_inc(y2_gated, 1)
                if on(i, at):
                    gate_num(0)
                if on(i, pr):
                    negative(1)
                if on(i, at):
                    gate_num(1)
                if on(i, nxt):
                    normalise(i, nxt, 0, x_in[:, nxt % 2], n1)
                if on(i, ff):
                    silu_gate(ff, 0)
                if on(i, pr):
                    elu_one(1)
                if on(i, ff):
                    silu_gate(ff, 1)
                if on(i, at):
                    dve.wait_ge(o_hi_made, upto(i, at))
                    nc.vector.tensor_tensor(o_lo[:], ps_tr, o_hi[:], ALU.subtract).then_inc(o_lo_made, 1)
                if on(i, ff):
                    silu_gate(ff, 2)
                if on(i, at):
                    dve.wait_ge(y_made, upto(i, at))
                    dve.wait_ge(xr_loaded[at % 2], 16 * (i + at // 2 + 1))
                    need(dve, out_made, upto(i, at) - 2)
                    nc.vector.scalar_tensor_tensor(x1[:, at % 2], ps_y, 1.0 / S_Y, x_res[:, at % 2], ALU.mult, ALU.add)\
                      .then_inc(x1_made, 1)
                    dve.wait_ge(x1_made, upto(i, at))
                    tile_stats(i, at, 1, x1[:, at % 2])
                    dve.wait_ge(ln_stats[1], TILES * upto(i, at))
                if on(i, nxt):
                    dve.wait_ge(n1_hi_made, upto(i, nxt))
                    nc.vector.tensor_tensor(n1_lo[:], ps_tr, n1_hi[:], ALU.subtract).then_inc(n1_lo_made, 1)
                if on(i, at):
                    mean_var(i, at, 1)

            steps(dve, step, setup)

        @block.tensor
        def _(pe):
            pe.wait_ge(s_wmod, 16)
            pe.wait_ge(silu_made, 1)
            for c in range(DC):
                for n, which in enumerate((0, 1, 3, 4)):
                    for kk in range(DC):
                        col = which * D + c * P
                        dst = bank[4][:, 0:DC * B * 4].rearrange("p (c b n) -> p c b n", c=DC, b=B)[:, c, :, n]
                        last = nc.tensor.matmul(dst, wmod[:, kk, col:col + P], silu_c[:, kk],
                                                start=kk == 0, stop=kk == DC - 1)
            last.then_inc(mod_cols, 1)
            pe.wait_ge(silu_rows_made, 1)
            for b in range(B):
                for kk in range(DC):
                    rhs = wmod[:, kk].rearrange("p (n d) -> p n d", n=6)[:, 2::3, :]
                    last = nc.tensor.matmul(bank[2 + b][:, :].rearrange("p (n d) -> p n d", n=2), silu_rows[:, kk, b], rhs,
                                            start=kk == 0, stop=kk == DC - 1)
                last.then_inc(mod_rows, 1)
            pe.wait_ge(sa_made, 2)
            pe.wait_ge(s_wa, 16)
            pe.wait_ge(const_made, 5)
            for half in range(2):
                cols = slice(512 * half, 512 * (half + 1))
                for c in range(DC):
                    nc.tensor.matmul(bank[half][:], sa_rows[:, c], wa32[:, c, cols], start=c == 0, stop=False)
                nc.tensor.matmul(bank[half][:], ones[:], ba[:, cols], start=False, stop=True).then_inc(bias_sum, 1)

            def setup(t):
                if t == -1:
                    pe.wait_ge(wa_lo_made, B * DC)
                    pe.wait_ge(bias_lo, 2 * B)
                    pe.wait_ge(picks_made, 4 * B)
                if t == 0:
                    pe.wait_ge(abs_added, 1)
                    nc.tensor.matmul(bank[0][:, 0:3], mean_mat[:], scale3[:], start=True, stop=True).then_inc(scale_sum, 1)
                    pe.wait_ge(wo_lo_made, B)
                    pe.wait_ge(bo_lo_made, 2)
                if t == 1:
                    pe.wait_ge(ternary_made, 3)
                    pe.wait_ge(gb_made, 1)

            def turn(src):
                for s in range(TILES):
                    for c in range(DC):
                        last = nc.tensor.transpose(ps_tr[:, c, s * P:(s + 1) * P], src[:, s, c * P:(c + 1) * P], ident[:])
                return last

            def step(i, k):
                nxt, pr, at, ff, dn = k + 1, k, k - 1, k - 2, k - 3

                def project(s, cols, dst, b, sig):
                    toks = slice(s * P, (s + 1) * P)
                    for c in range(DC):
                        nc.tensor.matmul(dst[:], n1_hi[:, c, toks], wa_hi[:, b, c, cols], start=c == 0, stop=False)
                        nc.tensor.matmul(dst[:], n1_hi[:, c, toks], wa_lo[:, b, c, cols], start=False, stop=False)
                        nc.tensor.matmul(dst[:], n1_lo[:, c, toks], wa_hi[:, b, c, cols], start=False, stop=False)
                    nc.tensor.matmul(dst[:], pick_a[:, b], bias_a[:, cols], start=False, stop=True).then_inc(sig, 1)

                def project_qk(s):
                    if s == 0:
                        need(pe, x1_made, upto(i, pr - 2))
                        pe.wait_ge(n1_lo_made, upto(i, pr))
                    else:
                        pe.wait_ge(rope_multiplied, TILES * (upto(i, pr) - 1) + 1)
                    project(s, slice(0, 2 * D), ps_qk, pr % 2, qk_projected)

                def project_vg(s):
                    if s == 0:
                        need(pe, y2_gated, upto(i, dn))
                    else:
                        pe.wait_ge(gate_made, TILES * (upto(i, pr) - 1) + 1)
                    project(s, slice(2 * D, 4 * D), ps_vg, pr % 2, vg_projected)

                def sum_kv(c):
                    s, r = c // 2, slice(CS * (c % 2), CS * (c % 2 + 1))
                    if c == 0:
                        need(pe, num_gated, TILES * (upto(i, at) - 1) - 1)
                        pe.wait_ge(v_copied, TILES * upto(i, at))
                    else:
                        pe.wait_ge(kv_masked, CH * (upto(i, at) - 1) + c)
                    for h in range(2):
                        last = nc.tensor.matmul(ps_kv[:, h], qk[r, at % 2, s, D + h * P:D + (h + 1) * P],
                                                v_ext[r, at % 2, s, h], start=c == 0 and h == 0, stop=c == CH - 1,
                                                skip_group_check=True)
                    last.then_inc(kv_summed, 1)

                def numerator(s):
                    if s == 0:
                        pe.wait_ge(q_copied, upto(i, at))
                        pe.wait_ge(kv_masked, CH * upto(i, at))
                    else:
                        need(pe, rope_multiplied, TILES * upto(i, pr))
                    pe.wait_ge(state_made, CH * (upto(i, at) - 1) + 2 * s + 2)
                    for c in (2 * s, 2 * s + 1):
                        r = CS * (c % 2)
                        for h in range(2):
                            last = nc.tensor.matmul(ps_num[s][r:r + CS, h], q_t[:, h, c * CS:(c + 1) * CS],
                                                    state[:, at % 2, c, h], start=True, stop=True)
                    last.then_inc(num_made, 1)

                def up_gate(p):
                    n = PAIRS * (upto(i, ff) - 1) + p + 1
                    if p == 0:
                        pe.wait_ge(h2_lo_made, upto(i, ff))
                    need(pe, hid_made, n - 2)
                    for dst, w, sig in ((ps_up[p % 2], w_up3, up_made), (ps_gate[p % 2], w_gate3, gate_up_made)):
                        for e in range(2):
                            ee = slice((2 * p + e) * P, (2 * p + e + 1) * P)
                            for c in range(DC):
                                nc.tensor.matmul(dst[:, e], w[:, c, ee], h2_hi[:, c], start=c == 0, stop=False)
                                last = nc.tensor.matmul(dst[:, e], w[:, c, ee], h2_lo[:, c], start=False, stop=c == DC - 1)
                        last.then_inc(sig, 1)

                def down(s):
                    if s == 0:
                        pe.wait_ge(hid_lo_made, PAIRS * upto(i, dn) - 1)
                        need(pe, gate_made, TILES * upto(i, pr - 1))
                    toks = slice(s * P, (s + 1) * P)
                    for e in range(EC):
                        if s == 0 and e == EC - 2:
                            pe.wait_ge(hid_lo_made, PAIRS * upto(i, dn))
                        nc.tensor.matmul(ps_y2[:, s], hid_hi[:, dn % 2, e, toks], w_down3[:, e], start=e == 0, stop=False)
                        last = nc.tensor.matmul(ps_y2[:, s], hid_lo[:, dn % 2, e, toks], w_down3[:, e],
                                                start=False, stop=e == EC - 1)
                    if s == TILES - 1:
                        last.then_inc(y2_made, 1)

                if on(i, at):
                    pe.wait_ge(qk_made, TILES * upto(i, at))
                    need(pe, n1_lo_made, upto(i, pr))
                    turn(qk[:, at % 2]).then_inc(q_turned, 1)
                    sum_kv(0)
                if on(i, pr):
                    project_qk(0)
                if on(i, at):
                    sum_kv(1)
                if on(i, dn):
                    down(0)
                if on(i, at):
                    sum_kv(2)
                if on(i, pr):
                    project_qk(1)
                if on(i, at):
                    sum_kv(3)
                if on(i, ff):
                    pe.wait_ge(ln_done[1], TILES * upto(i, ff))
                    need(pe, q_copied, upto(i, at))
                    turn(n2).then_inc(n2_turned, 1)
                if on(i, dn):
                    down(1)
                if on(i, at):
                    numerator(0)
                    numerator(1)
                if on(i, ff):
                    up_gate(0)
                if on(i, pr):
                    project_vg(0)
                if on(i, ff):
                    up_gate(1)
                if on(i, at):
                    pe.wait_ge(o_made, TILES * upto(i, at))
                    need(pe, h2_made, DC * upto(i, ff))
                    turn(o).then_inc(o_turned, 1)
                if on(i, pr):
                    project_vg(1)
                if on(i, ff):
                    up_gate(2)
                if on(i, at):
                    pe.wait_ge(o_lo_made, upto(i, at))
                    pe.wait_ge(num_gated, TILES * upto(i, at))
                    for s in range(TILES):
                        toks = slice(s * P, (s + 1) * P)
                        for c in range(DC):
                            nc.tensor.matmul(ps_y[:, s], o_hi[:, c, toks], wo_hi[:, at % 2, c], start=c == 0, stop=False)
                            nc.tensor.matmul(ps_y[:, s], o_hi[:, c, toks], wo_lo[:, at % 2, c], start=False, stop=False)
                            nc.tensor.matmul(ps_y[:, s], o_lo[:, c, toks], wo_hi[:, at % 2, c], start=False, stop=False)
                        last = nc.tensor.matmul(ps_y[:, s], pick_o[:, at % 2], bias_o[:], start=False, stop=True)
                    last.then_inc(y_made, 1)
                if on(i, nxt):
                    pe.wait_ge(ln_done[0], TILES * upto(i, nxt))
                    need(pe, o_lo_made, upto(i, at))
                    turn(n1).then_inc(n1_turned, 1)
                if on(i, ff):
                    up_gate(3)

            steps(pe, step, setup)


def kernel(**inputs):
    import concourse.bacc as bacc
    from concourse.bass_utils import run_bass_kernel_spmd

    a = {k.replace("L0_", ""): np.asarray(v) for k, v in inputs.items()}
    rope, mask, ident = constants()
    arrays = {
        "x": a["attn_x"],
        "w_attn": np.concatenate([a[f"attn_W{n}"].T for n in "qkvg"], 1),
        "w_out": a["attn_Wo"].T,
        "b_attn": np.concatenate([a[f"attn_b{n}"] for n in "qkvg"])[None],
        "b_out": a["attn_bo"][None],
        "w_up": a["ffn_W_up"].T,
        "w_gate": a["ffn_W_gate"].T,
        "w_down": a["ffn_W_down"].T,
        "c_t": a["c"].T,
        "w_mod": a["wmod"],
        "rope_t": rope.reshape(T // GT, P, TILES * 2 * DK),
        "mask_t": mask,
        "ident_t": ident,
    }
    arrays = {k: np.ascontiguousarray(v) for k, v in arrays.items()}
    nc = bacc.Bacc("TRN2", target_bir_lowering=False, num_devices=1)
    args = [nc.dram_tensor(f"in_{k}", v.shape, F32, kind="ExternalInput").ap() for k, v in arrays.items()]
    out = nc.dram_tensor("block_out", (B, T, D), F32, kind="ExternalOutput").ap()
    block_kernel(nc, *args, out)
    r = run_bass_kernel_spmd(nc, [{f"in_{k}": v for k, v in arrays.items()}], core_ids=[0])
    return r.results[0]["block_out"]
```

```python
import numpy as np
import concourse.bass as bass
from concourse import mybir
from contextlib import ExitStack

F32 = mybir.dt.float32
F16 = mybir.dt.float16
ALU = mybir.AluOpType
ACT = mybir.ActivationFunctionType

P = 128
B, T, D = 2, 2048, 256
H = 16
DK = D // H
CS = 64
E = 1024
DC = D // P
EC = E // P
TILES = 2
GT = TILES * P
CH = GT // CS
GROUPS = B * T // GT
FIRST = 5
ABS_CUTS = 2
WARM_UP = 12
PAIRS = EC // 2
HH = P // DK
VW = P + HH

LN_EPS = 1e-5
Q_EPS = 1e-8
DEN_EPS = 1e-6

S_N = 2.0 ** 5
S_W = 2.0 ** 10
S_O = 2.0 ** 4
S_H = 2.0 ** -7
S_QKVG = S_N * S_W
S_Y = S_O * S_W


def constants():
    inv = np.float32(1.0) / np.power(np.float32(10000.0), np.arange(0, DK, 2, dtype=np.float32) / np.float32(DK))
    ang = np.arange(T, dtype=np.float32)[:, None] * inv[None]
    cos, sin = np.cos(ang), np.sin(ang)
    rope = np.empty((T, 2, DK // 2, 2), np.float32)
    rope[:, 0, :, 0] = cos
    rope[:, 0, :, 1] = cos
    rope[:, 1, :, 0] = -sin
    rope[:, 1, :, 1] = sin
    rope *= np.float32(1.0 / S_QKVG)
    rope = rope.reshape(T // GT, TILES, P, 2 * DK).transpose(0, 2, 1, 3).copy()
    head = np.arange(P) // DK
    mask = np.concatenate([head[:, None] == head[None, :], head[:, None] == np.arange(HH)[None, :]], 1)
    mask = np.stack([mask] * 2, 1).astype(np.float32)
    return rope, mask, np.eye(P, dtype=np.float32)


def block_kernel(nc, x, w_attn, w_out, b_attn, b_out, w_up, w_gate, w_down, c_t, w_mod,
                 rope_t, mask_t, ident_t, batch_t, out):
    ctx = ExitStack()
    with ctx:
        def sb(name, shape, dt=F32):
            return ctx.enter_context(nc.sbuf_tensor(name, shape, dt))

        def sem(name):
            return ctx.enter_context(nc.semaphore(name))

        ident = sb("ident", [P, P])
        mask = sb("mask", [P, 2, VW])
        c_sb = sb("c_sb", [P, DC, B])
        c_th = sb("c_th", [P, DC, B])
        silu_c = sb("silu_c", [P, DC, B])
        batch_rows = sb("batch_rows", [B, B, P])
        wmod = sb("wmod", [P, DC, 6 * D])
        wa32 = sb("wa32", [P, DC, 4 * D])
        wo32 = sb("wo32", [P, DC, D])
        wf32 = sb("wf32", [P, 3, DC * E])
        ba = sb("ba", [1, 4 * D])
        bo_rows = sb("bo_rows", [P, D])
        ones = sb("ones", [1, P])
        mean_mat = sb("mean_mat", [P, P])
        shift = sb("shift", [P, DC, B, 4])
        sa_rows = sb("sa_rows", [P, DC, 2, B, 32])
        ca_scale = sb("ca_scale", [P, DC, B])
        cb_scale = sb("cb_scale", [P, DC, B])
        sb_shift = sb("sb_shift", [P, DC, B])
        gates = sb("gates", [B, 2 * D])
        gate_sign = sb("gate_sign", [B, 2 * D])
        gate_abs = sb("gate_abs", [B, 2 * D])
        gb_scaled = sb("gb_scaled", [P, B, D])
        bo_scaled = sb("bo_scaled", [P, D])
        wa_hi = sb("wa_hi", [P, B, DC, 4 * D], F16)
        wa_lo = sb("wa_lo", [P, B, DC, 4 * D], F16)
        wo_hi = sb("wo_hi", [P, B, DC, D], F16)
        wo_lo = sb("wo_lo", [P, B, DC, D], F16)
        bias_a = sb("bias_a", [P, 4 * D], F16)
        bias_o = sb("bias_o", [P, D], F16)
        pick_a = sb("pick_a", [P, B, P], F16)
        pick_o = sb("pick_o", [P, B, P], F16)
        abs_sums = sb("abs_sums", [P, 3, ABS_CUTS])
        scale3 = sb("scale3", [P, 3])
        thr = sb("thr", [P, 2, 3])
        tanh_scale = sb("tanh_scale", [P, 1])
        prod3 = sb("prod3", [P, 2])
        ga_rows = sb("ga_rows", [P, B, D])
        w3 = sb("w3", [P, 3, DC * E], F16)
        w_up3 = w3[:, 0, :].rearrange("p (c e) -> p c e", c=DC)
        w_gate3 = w3[:, 1, :].rearrange("p (c e) -> p c e", c=DC)
        w_down3 = w3[:, 2, :].rearrange("p (e d) -> p e d", e=EC)
        minus_half = sb("minus_half", [P, TILES])

        x_in = sb("x_in", [P, 2, TILES, D])
        x_res = sb("x_res", [P, 2, TILES, D])
        rope = sb("rope", [P, 2, TILES, 2 * DK])
        stats = sb("stats", [P, 2, TILES, 6])
        mv = sb("mv", [P, 2, TILES, 2])
        var_s = sb("var_s", [P, 2, TILES])
        rstd = sb("rstd", [P, 2, TILES])
        n1 = sb("n1", [P, TILES, D])
        n1_hi = sb("n1_hi", [P, DC, GT], F16)
        n1_lo = sb("n1_lo", [P, DC, GT], F16)
        rot = sb("rot", [P, TILES, 2 * D])
        neg = sb("neg", [P, TILES, 2 * D])
        qk = sb("qk", [P, 2, TILES, 2 * D])
        v_ext = sb("v_ext", [P, 2, TILES, 2, VW])
        gate_t = sb("gate_t", [P, 2, TILES, D])
        q_t = sb("q_t", [P, DC, GT])
        kv_m = sb("kv_m", [P, CH, 2, VW])
        state = sb("state", [P, B, CH, 2, VW])
        den = sb("den", [P, TILES, H])
        rden = sb("rden", [P, TILES, H])
        gated = sb("gated", [P, TILES, D])
        o = sb("o", [P, TILES, D])
        o_hi = sb("o_hi", [P, DC, GT], F16)
        o_lo = sb("o_lo", [P, DC, GT], F16)
        x1 = sb("x1", [P, 2, TILES, D])
        n2 = sb("n2", [P, TILES, D])
        h2 = sb("h2", [P, DC, GT])
        h2_hi = sb("h2_hi", [P, DC, GT], F16)
        h2_lo = sb("h2_lo", [P, DC, GT], F16)
        hid = sb("hid", [P, PAIRS, 2, GT])
        hid_hi = sb("hid_hi", [P, 2, EC, GT], F16)
        hid_lo = sb("hid_lo", [P, 2, EC, GT], F16)
        y2g = sb("y2g", [P, TILES, D])
        out_sb = sb("out_sb", [P, 2, TILES, D])

        wo_scaled = [x1[:, b] for b in range(B)]
        below = [hid_hi[:, 1].rearrange("p e t -> p (e t)"), hid_lo[:, 1].rearrange("p e t -> p (e t)")]
        abs_junk = hid[:, 0:2].rearrange("p a b c -> p (a b c)")

        bank = [ctx.enter_context(nc.psum_tensor(f"bank{i}", [P, 512], F32)) for i in range(8)]
        ps_up = [bank[0][:, :].rearrange("p (e t) -> p e t", e=2), bank[2][:, :].rearrange("p (e t) -> p e t", e=2)]
        ps_gate = [bank[1][:, :].rearrange("p (e t) -> p e t", e=2), bank[3][:, :].rearrange("p (e t) -> p e t", e=2)]
        ps_tr = bank[4][:, :].rearrange("p (c t) -> p c t", c=DC)
        ps_qk = bank[5]
        ps_vg = bank[6]
        ps_kv = bank[7][:, 0:2 * VW].rearrange("p (h v) -> p h v", h=2)
        ps_num = [bank[7][:, 0:2 * VW].rearrange("p (h v) -> p h v", h=2),
                  bank[5][:, 0:2 * VW].rearrange("p (h v) -> p h v", h=2)]
        ps_y = bank[5][:, :].rearrange("p (s d) -> p s d", s=TILES)
        ps_mod = bank[7][:, 0:4 * DC * B].rearrange("p (c b n) -> p c b n", c=DC, b=B)
        ps_gates = [bank[2], bank[3]]
        ps_y2 = bank[6][:, :].rearrange("p (s d) -> p s d", s=TILES)

        s_c, s_ident, s_ba, s_mask, s_batch, s_wmod_a, s_wmod_b, s_wa, s_wo = [
            sem(f"{n}_loaded") for n in ("c", "ident", "b_attn", "mask", "batch_rows", "wmod_a", "wmod_b", "w_attn", "w_out")]
        s_wf = [sem(f"w_ffn{m}_loaded") for m in range(3)]
        x_loaded = [sem(f"x_loaded{i}") for i in range(2)]
        xr_loaded = [sem(f"xr_loaded{i}") for i in range(2)]
        rope_loaded = [sem(f"rope_loaded{i}") for i in range(2)]
        stored = [sem(f"stored{i}") for i in range(2)]
        c_tanh, silu_made = sem("c_tanh"), sem("silu_made")
        mod_cols, gate_rows, shift_made, sa_made = sem("mod_cols"), sem("gate_rows"), sem("shift_made"), sem("sa_made")
        ca_made, second_made, gates_spread = sem("ca_made"), sem("second_made"), sem("gates_spread")
        gates_part, gates_made = sem("gates_part"), sem("gates_made")
        bias_sum, bias_hi, bias_lo = sem("bias_sum"), sem("bias_hi"), sem("bias_lo")
        wa_hi_made, wa_lo_made, wo_scl, wo_hi_made, wo_lo_made = [
            sem(n) for n in ("wa_hi_made", "wa_lo_made", "wo_scl", "wo_hi_made", "wo_lo_made")]
        bo_scl, bo_hi_made, bo_lo_made = sem("bo_scl"), sem("bo_hi_made"), sem("bo_lo_made")
        abs_made, abs_added, scale_sum, scale_made, thr_made = [
            sem(n) for n in ("abs_made", "abs_added", "scale_sum", "scale_made", "thr_made")]
        below_made, ternary_made, gb_made = sem("below_made"), sem("ternary_made"), sem("gb_made")
        const_made, ga_spread = sem("const_made"), sem("ga_spread")
        picks_zeroed, picks_made = sem("picks_zeroed"), sem("picks_made")
        ln_stats = [sem(f"ln{i}_stats") for i in (1, 2)]
        ln_mv = [sem(f"ln{i}_mean_var") for i in (1, 2)]
        ln_var = [sem(f"ln{i}_var_scaled") for i in (1, 2)]
        ln_rstd = [sem(f"ln{i}_rstd") for i in (1, 2)]
        ln_done = [sem(f"ln{i}_normalised") for i in (1, 2)]
        n1_turned, n1_hi_made, n1_lo_made = sem("n1_turned"), sem("n1_hi_made"), sem("n1_lo_made")
        qk_projected, vg_projected = sem("qk_projected"), sem("vg_projected")
        rope_multiplied, rope_added, neg_made, exp_made, qk_made = [
            sem(n) for n in ("rope_multiplied", "rope_added", "neg_made", "exp_made", "qk_made")]
        v_copied, gate_made = sem("v_copied"), sem("gate_made")
        q_turned, q_copied = sem("q_turned"), sem("q_copied")
        kv_summed, kv_masked, state_made = sem("kv_summed"), sem("kv_masked"), sem("state_made")
        num_made, den_made, rden_made, num_gated, o_made = [
            sem(n) for n in ("num_made", "den_made", "rden_made", "num_gated", "o_made")]
        o_turned, o_hi_made, o_lo_made = sem("o_turned"), sem("o_hi_made"), sem("o_lo_made")
        y_made, x1_made = sem("y_made"), sem("x1_made")
        n2_turned, h2_made, h2_hi_made, h2_lo_made = [sem(n) for n in ("n2_turned", "h2_made", "h2_hi_made", "h2_lo_made")]
        up_made, gate_up_made, tanh_made, hid_part, hid_made, hid_hi_made, hid_lo_made = [
            sem(n) for n in ("up_made", "gate_up_made", "tanh_made", "hid_part", "hid_made", "hid_hi_made", "hid_lo_made")]
        y2_made, y2_gated, out_made = sem("y2_made"), sem("y2_gated"), sem("out_made")

        block = ctx.enter_context(nc.Block())

        x_v = x.rearrange("b (g s p) d -> b g p s d", s=TILES, p=P)
        out_v = out.rearrange("b (g s p) d -> b g p s d", s=TILES, p=P)

        def need(eng, semaphore, value):
            if not isinstance(value, int) or value > 0:
                eng.wait_ge(semaphore, value)

        def on(i, g):
            return not isinstance(i, int) or 0 <= g < GROUPS

        def upto(i, g):
            return 2 * i + g + 1 if not isinstance(i, int) else max(0, min(g + 1, GROUPS))

        def steps(eng, step):
            for t in range(-1, FIRST):
                step(0, t)
            with eng.Fori(0, (GROUPS - 1 - FIRST) // 2) as i:
                step(i, FIRST)
                step(i, FIRST + 1)
            for t in range(GROUPS - 1, GROUPS + 3):
                step(0, t)

        @block.sync
        def _(sp):
            def load_x(i, g):
                need(sp, ln_done[0], TILES * upto(i, g - 2))
                sp.dma_start(x_in[:, g % 2], x_v[g % 2, i + g // 2]).then_inc(x_loaded[g % 2], 16)

            def load_rope(i, g):
                need(sp, rope_multiplied, TILES * upto(i, g - 2))
                sp.dma_start(rope[:, g % 2], rope_t[i + g // 2].rearrange("p (s c) -> p s c", s=TILES))\
                  .then_inc(rope_loaded[g % 2], 16)

            sp.dma_start(c_sb[:], c_t.rearrange("(k p) b -> p k b", p=P)).then_inc(s_c, 16)
            wmod_v = w_mod.rearrange("(k p) n -> p k n", p=P)
            sp.dma_start(wmod[:, :, 0:2 * D], wmod_v[:, :, 0:2 * D]).then_inc(s_wmod_a, 16)
            load_x(0, 0)
            sp.dma_start(ident[:], ident_t).then_inc(s_ident, 16)
            sp.dma_start(wa32[:], w_attn.rearrange("(c p) n -> p c n", p=P)).then_inc(s_wa, 16)
            sp.dma_start(ba[:], b_attn).then_inc(s_ba, 16)
            load_rope(0, 0)
            sp.dma_start(wmod[:, :, 2 * D:6 * D], wmod_v[:, :, 2 * D:6 * D]).then_inc(s_wmod_b, 16)
            load_x(0, 1)
            sp.dma_start(mask[:], mask_t).then_inc(s_mask, 16)
            sp.dma_start(batch_rows[:], batch_t).then_inc(s_batch, 16)
            sp.dma_start(wo32[:], w_out.rearrange("(c p) n -> p c n", p=P)).then_inc(s_wo, 16)
            sp.dma_start(bo_rows[:], b_out.broadcast_to([P, D])).then_inc(s_wo, 16)
            sp.dma_start(wf32[:, 0].rearrange("p (c e) -> p c e", c=DC), w_up.rearrange("(c p) e -> p c e", p=P)).then_inc(s_wf[0], 16)
            sp.dma_start(wf32[:, 1].rearrange("p (c e) -> p c e", c=DC), w_gate.rearrange("(c p) e -> p c e", p=P)).then_inc(s_wf[1], 16)
            sp.dma_start(wf32[:, 2].rearrange("p (e d) -> p e d", e=EC), w_down.rearrange("(e p) d -> p e d", p=P)).then_inc(s_wf[2], 16)

            def step(i, k):
                if on(i, k + 1) and k >= 1:
                    load_x(i, k + 1)
                if on(i, k + 1) and k >= 0:
                    load_rope(i, k + 1)
                if on(i, k):
                    need(sp, x1_made, upto(i, k - 2))
                    sp.dma_start(x_res[:, k % 2], x_v[k % 2, i + k // 2]).then_inc(xr_loaded[k % 2], 16)
                if on(i, k - 3):
                    d = k - 3
                    sp.wait_ge(out_made, upto(i, d))
                    sp.dma_start(out_v[d % 2, i + d // 2], out_sb[:, d % 2]).then_inc(stored[d % 2], 16)

            steps(sp, step)
            for p in range(2):
                sp.wait_ge(stored[p], 16 * (GROUPS // 2))

        @block.gpsimd
        def _(pool):
            nc.gpsimd.memset(ones[:], 1.0).then_inc(const_made, 1)
            nc.gpsimd.memset(mean_mat[:], 1.0 / (D * E)).then_inc(const_made, 1)
            nc.gpsimd.memset(minus_half[:], -0.5).then_inc(const_made, 1)
            nc.gpsimd.memset(pick_a[:], 0.0).then_inc(picks_zeroed, 1)
            nc.gpsimd.memset(pick_o[:], 0.0).then_inc(picks_zeroed, 1)
            nc.gpsimd.memset(state[:, :, CH - 1], 0.0).then_inc(const_made, 1)
            nc.gpsimd.memset(v_ext[:, :, :, :, P:VW], 1.0).then_inc(const_made, 1)
            pool.wait_ge(picks_zeroed, 2)
            pool.wait_ge(const_made, 5)
            n = 0
            for b in range(B):
                for pick, value, rows in ((pick_a, S_N, (32 * b, 64 + 32 * b)), (pick_o, 2 * S_O, (64 * b, 64 * b + 32))):
                    for row in rows:
                        need(pool, picks_made, n)
                        nc.gpsimd.memset(pick[row:row + 1, b, :], value).then_inc(picks_made, 1)
                        n += 1
            pool.wait_ge(picks_made, n)

            def inverse_std(i, g, which):
                pool.wait_ge(ln_var[which], upto(i, g))
                nc.gpsimd.tensor_tensor(rstd[:, which], var_s[:, which], minus_half[:], ALU.pow)\
                  .then_inc(ln_rstd[which], 1)

            def setup(place):
                if place == "output weights":
                    pool.wait_ge(s_wo, 32)
                    for b in range(B):
                        pool.wait_ge(ga_spread, b + 1)
                        nc.gpsimd.tensor_tensor(wo_scaled[b], wo32[:], ga_rows[:, b:b + 1].broadcast_to([P, DC, D]), ALU.mult)\
                          .then_inc(wo_scl, 1)
                if place == "output split":
                    for b in range(B):
                        pool.wait_ge(wo_hi_made, b + 1)
                        nc.gpsimd.tensor_tensor(wo_lo[:, b], wo_scaled[b], wo_hi[:, b], ALU.subtract).then_inc(wo_lo_made, 1)

            def step(i, k):
                nxt, pr, at, ff, dn = k + 1, k, k - 1, k - 2, k - 3

                def add_state(c):
                    pool.wait_ge(kv_masked, CH * (upto(i, at) - 1) + c + 1)
                    nc.gpsimd.tensor_tensor(state[:, at % 2, c], state[:, at % 2, CH - 1], kv_m[:, c], ALU.add)\
                      .then_inc(state_made, 1)

                def add_rope(s):
                    pool.wait_ge(rope_multiplied, TILES * (upto(i, pr) - 1) + s + 1)
                    nc.gpsimd.tensor_tensor(rot[:, s], rot[:, s], neg[:, s], ALU.add).then_inc(rope_added, 1)

                def split_hidden(f, p):
                    pool.wait_ge(hid_hi_made, PAIRS * (upto(i, f) - 1) + p + 1)
                    nc.gpsimd.tensor_tensor(hid_lo[:, f % 2, 2 * p:2 * p + 2], hid[:, p],
                                            hid_hi[:, f % 2, 2 * p:2 * p + 2], ALU.subtract).then_inc(hid_lo_made, 1)

                def divide(s):
                    pool.wait_ge(num_gated, TILES * (upto(i, at) - 1) + s + 1)
                    nc.gpsimd.tensor_tensor(o[:, s].rearrange("p (h e) -> p h e", h=H),
                                            gated[:, s].rearrange("p (h e) -> p h e", h=H),
                                            rden[:, s].unsqueeze(2).broadcast_to([P, H, DK]), ALU.mult)\
                      .then_inc(o_made, 1)

                if on(i, at):
                    add_state(0)
                if on(i, dn):
                    split_hidden(dn, PAIRS - 1)
                if k == 0:
                    inverse_std(i, nxt, 0)
                if on(i, pr):
                    add_rope(0)
                if k == 1:
                    setup("output weights")
                if on(i, at):
                    add_state(1)
                    add_state(2)
                    add_state(3)
                if on(i, pr):
                    add_rope(1)
                if k == 1:
                    setup("output split")
                if on(i, nxt) and k != 0:
                    inverse_std(i, nxt, 0)
                if on(i, dn):
                    pool.wait_ge(y2_gated, upto(i, dn))
                    need(pool, stored[dn % 2], 16 * (i + dn // 2))
                    nc.gpsimd.tensor_tensor(out_sb[:, dn % 2], y2g[:], x1[:, dn % 2], ALU.add).then_inc(out_made, 1)
                if on(i, at):
                    divide(0)
                    divide(1)
                if on(i, ff):
                    split_hidden(ff, 0)
                    split_hidden(ff, 1)
                    split_hidden(ff, 2)
                if on(i, at):
                    inverse_std(i, at, 1)

            steps(pool, step)

        @block.scalar
        def _(act):
            act.wait_ge(s_c, 16)
            nc.scalar.activation(c_th[:], c_sb[:], ACT.Tanh, scale=0.5).then_inc(c_tanh, 1)

            def sum_abs(m):
                act.wait_ge(s_wf[m], 16)
                width = DC * E // ABS_CUTS
                for q in range(ABS_CUTS):
                    need(act, abs_made, ABS_CUTS * m + q)
                    nc.scalar.activation(abs_junk[:, 0:width], wf32[:, m, width * q:width * (q + 1)], ACT.Abs,
                                         accum_out=abs_sums[:, m, q:q + 1]).then_inc(abs_made, 1)

            def setup(place):
                if place == "norm turned":
                    act.wait_ge(ca_made, 1)
                    act.wait_ge(s_wa, 16)
                    for c in range(DC):
                        nc.scalar.activation(wa_hi[:, 0, c], wa32[:, c], ACT.Copy, scale=ca_scale[:, c, 0:1])\
                          .then_inc(wa_hi_made, 1)
                    for half in range(2):
                        act.wait_ge(bias_sum, half + 1)
                        nc.scalar.activation(bias_a[:, 512 * half:512 * (half + 1)], bank[half][:], ACT.Copy, scale=S_W)\
                          .then_inc(bias_hi, 1)
                        nc.scalar.activation(wa_hi[:, 1, half], wa32[:, half], ACT.Copy, scale=ca_scale[:, half, 1:2])\
                          .then_inc(wa_hi_made, 1)
                if place == "first exp":
                    sum_abs(0)
                    sum_abs(1)
                if place == "sums":
                    sum_abs(2)
                if place == "output weights":
                    for b in range(B):
                        act.wait_ge(gates_spread, b + 1)
                        nc.scalar.activation(ga_rows[:, b], ps_gates[b][:, 0:D], ACT.Copy, scale=0.25 * S_W).then_inc(ga_spread, 1)
                if place == "output split":
                    for b in range(B):
                        act.wait_ge(wo_scl, b + 1)
                        nc.scalar.activation(wo_hi[:, b], wo_scaled[b], ACT.Copy).then_inc(wo_hi_made, 1)
                    act.wait_ge(bo_scl, 2)
                    nc.scalar.activation(bias_o[:], bo_scaled[:], ACT.Copy).then_inc(bo_hi_made, 1)
                if place == "down gates":
                    act.wait_ge(thr_made, 5)
                    for b in range(B):
                        nc.scalar.activation(gb_scaled[:, b], ps_gates[b][:, D:2 * D], ACT.Copy, scale=prod3[:, 1:2]).then_inc(gb_made, 1)

            def step(i, k):
                nxt, pr, at, ff, dn = k + 1, k, k - 1, k - 2, k - 3

                def keys_exp(s):
                    act.wait_ge(neg_made, TILES * (upto(i, pr) - 1) + s + 1)
                    nc.scalar.activation(neg[:, s], neg[:, s], ACT.Exp).then_inc(exp_made, 1)

                def values_and_gate(s):
                    n = TILES * (upto(i, pr) - 1) + s + 1
                    act.wait_ge(vg_projected, n)
                    nc.scalar.activation(v_ext[:, pr % 2, s, :, 0:P],
                                         ps_vg[:, 0:D].rearrange("p (h v) -> p h v", h=2), ACT.Copy,
                                         scale=S_O / S_QKVG).then_inc(v_copied, 1)
                    nc.scalar.activation(gate_t[:, pr % 2, s], ps_vg[:, D:2 * D], ACT.Tanh,
                                         scale=0.5 / S_QKVG).then_inc(gate_made, 1)

                def tanh_up(p):
                    n = PAIRS * (upto(i, ff) - 1) + p + 1
                    act.wait_ge(up_made, n)
                    need(act, hid_lo_made, n - PAIRS)
                    nc.scalar.activation(hid[:, p], ps_up[p % 2], ACT.Tanh, scale=tanh_scale[:, 0:1])\
                      .then_inc(tanh_made, 1)

                def hidden_high(f, p):
                    act.wait_ge(hid_made, PAIRS * (upto(i, f) - 1) + p + 1)
                    nc.scalar.activation(hid_hi[:, f % 2, 2 * p:2 * p + 2], hid[:, p], ACT.Copy)\
                      .then_inc(hid_hi_made, 1)

                if on(i, at):
                    act.wait_ge(q_turned, upto(i, at))
                    nc.scalar.activation(q_t[:], ps_tr, ACT.Copy).then_inc(q_copied, 1)
                if on(i, dn):
                    hidden_high(dn, PAIRS - 1)
                if on(i, pr):
                    keys_exp(0)
                if on(i, pr):
                    if k < 3:
                        values_and_gate(0)
                if k == 0:
                    setup("first exp")
                if k == 1:
                    setup("down gates")
                if on(i, ff):
                    act.wait_ge(n2_turned, upto(i, ff))
                    for c in range(DC):
                        nc.scalar.activation(h2[:, c], ps_tr[:, c], ACT.Identity,
                                             scale=cb_scale[:, c, ff % 2:ff % 2 + 1],
                                             bias=sb_shift[:, c, ff % 2:ff % 2 + 1]).then_inc(h2_made, 1)
                    act.wait_ge(h2_made, DC * upto(i, ff))
                    nc.scalar.activation(h2_hi[:], h2[:], ACT.Copy).then_inc(h2_hi_made, 1)
                if on(i, pr):
                    keys_exp(1)
                if on(i, ff):
                    tanh_up(0)
                if on(i, pr):
                    if k < 3:
                        values_and_gate(1)
                    else:
                        values_and_gate(0)
                if k == 1:
                    setup("output split")
                if on(i, ff):
                    hidden_high(ff, 0)
                    tanh_up(1)
                if on(i, at):
                    act.wait_ge(o_turned, upto(i, at))
                    nc.scalar.activation(o_hi[:], ps_tr, ACT.Copy).then_inc(o_hi_made, 1)
                if on(i, ff):
                    hidden_high(ff, 1)
                if on(i, pr) and k >= 3:
                    values_and_gate(1)
                if on(i, ff):
                    tanh_up(2)
                    hidden_high(ff, 2)
                if on(i, nxt):
                    act.wait_ge(n1_turned, upto(i, nxt))
                    nc.scalar.activation(n1_hi[:], ps_tr, ACT.Copy).then_inc(n1_hi_made, 1)
                if k == -1:
                    setup("norm turned")
                if k == 0:
                    setup("output weights")
                    setup("sums")
                if on(i, ff):
                    tanh_up(3)

            steps(act, step)

        @block.vector
        def _(dve):
            dve.wait_ge(c_tanh, 1)
            nc.vector.scalar_tensor_tensor(silu_c[:], c_th[:], 1.0, c_sb[:], ALU.add, ALU.mult).then_inc(silu_made, 1)

            def weights_low(b, c):
                dve.wait_ge(wa_hi_made, DC * b + c + 1)
                nc.vector.scalar_tensor_tensor(wa_lo[:, b, c], wa32[:, c], ca_scale[:, c, b:b + 1], wa_hi[:, b, c],
                                               ALU.mult, ALU.subtract).then_inc(wa_lo_made, 1)

            def less(m):
                dve.wait_ge(thr_made, 4)
                need(dve, ternary_made, m - 1)
                nc.vector.tensor_scalar(below[m % 2], wf32[:, m], thr[:, 1, m:m + 1], None, ALU.is_lt).then_inc(below_made, 1)

            def ternary(m):
                dve.wait_ge(below_made, m + 1)
                nc.vector.scalar_tensor_tensor(w3[:, m], wf32[:, m], thr[:, 0, m:m + 1], below[m % 2],
                                               ALU.is_gt, ALU.subtract).then_inc(ternary_made, 1)

            def setup(place):
                if place == "normalised":
                    dve.wait_ge(mod_cols, 1)
                    nc.vector.tensor_scalar(shift[:, :, :, 0:2], ps_mod[:, :, :, 0:2], 0.5, None, ALU.mult).then_inc(shift_made, 1)
                    dve.wait_ge(shift_made, 1)
                    nc.vector.tensor_scalar(ca_scale[:], shift[:, :, :, 1], 1.0, S_W, ALU.add, ALU.mult).then_inc(ca_made, 1)
                    for b in range(B):
                        nc.vector.tensor_copy(sa_rows[:, :, :, b], shift[:, :, b, 0:1].unsqueeze(3)
                                              .broadcast_to([P, DC, 2, 32])).then_inc(sa_made, 1)
                if place == "norm split":
                    dve.wait_ge(ca_made, 1)
                    dve.wait_ge(s_wa, 16)
                    for c in range(DC):
                        weights_low(0, c)
                if place == "bias":
                    for half in range(2):
                        cols = slice(512 * half, 512 * (half + 1))
                        dve.wait_ge(bias_hi, half + 1)
                        nc.vector.scalar_tensor_tensor(bias_a[64:P, cols], bank[half][64:P, :], S_W, bias_a[64:P, cols],
                                                       ALU.mult, ALU.subtract).then_inc(bias_lo, 1)
                        if half == 0:
                            weights_low(1, 0)
                if place == "gate rows":
                    dve.wait_ge(gate_rows, 1)
                    nc.vector.tensor_scalar(gate_sign[:], bank[3][0:B, :], 0.0, 2.0, ALU.is_ge, ALU.mult).then_inc(gates_part, 1)
                    dve.wait_ge(gates_part, 1)
                    nc.vector.scalar_tensor_tensor(gate_abs[:], gate_sign[:], 1.0, bank[3][0:B, :], ALU.subtract, ALU.mult)\
                      .then_inc(gates_part, 1)
                if place == "gate rows sign":
                    dve.wait_ge(gates_part, 2)
                    nc.vector.tensor_scalar(gate_sign[:], gate_sign[:], 1.0, None, ALU.subtract).then_inc(gates_part, 1)
                    dve.wait_ge(gates_part, 3)
                    nc.vector.scalar_tensor_tensor(gates[:], gate_abs[:], 0.5, gate_sign[:], ALU.max, ALU.mult).then_inc(gates_made, 1)
                if place == "second columns":
                    dve.wait_ge(mod_cols, 2)
                    nc.vector.tensor_scalar(cb_scale[:], ps_mod[:, :, :, 3], 0.5, 1.0, ALU.mult, ALU.add).then_inc(second_made, 1)
                    nc.vector.tensor_scalar(sb_shift[:], ps_mod[:, :, :, 2], 0.5 * S_N, None, ALU.mult).then_inc(second_made, 1)
                if place == "output bias":
                    dve.wait_ge(ga_spread, B)
                    dve.wait_ge(s_wo, 32)
                    for b in range(B):
                        r = slice(64 * b, 64 * b + 64)
                        nc.vector.tensor_tensor(bo_scaled[r], bo_rows[r], ga_rows[r, b], ALU.mult).then_inc(bo_scl, 1)
                if place == "output bias low":
                    dve.wait_ge(bo_hi_made, 1)
                    for b in range(B):
                        r = slice(64 * b + 32, 64 * b + 64)
                        nc.vector.tensor_tensor(bias_o[r], bo_scaled[r], bias_o[r], ALU.subtract).then_inc(bo_lo_made, 1)
                if place == "sums":
                    dve.wait_ge(abs_made, 3 * ABS_CUTS)
                    nc.vector.tensor_reduce(scale3[:], abs_sums[:], axis=mybir.AxisListType.X, op=ALU.add).then_inc(abs_added, 1)
                    dve.wait_ge(s_mask, 16)
                if place == "scales":
                    dve.wait_ge(scale_sum, 1)
                    nc.vector.tensor_scalar(scale3[:], bank[0][:, 0:3], Q_EPS, None, ALU.add).then_inc(scale_made, 1)
                    dve.wait_ge(scale_made, 1)
                    nc.vector.tensor_scalar(thr[:, 0], scale3[:], 0.5, None, ALU.mult).then_inc(thr_made, 1)
                    nc.vector.tensor_scalar(thr[:, 1], scale3[:], -0.5, None, ALU.mult).then_inc(thr_made, 1)
                    nc.vector.tensor_scalar(tanh_scale[:], scale3[:, 0:1], 0.5 / S_N, None, ALU.mult).then_inc(thr_made, 1)
                    nc.vector.tensor_tensor(prod3[:, 0:1], scale3[:, 0:1], scale3[:, 1:2], ALU.mult).then_inc(thr_made, 1)
                    dve.wait_ge(thr_made, 4)
                    nc.vector.scalar_tensor_tensor(prod3[:, 1:2], prod3[:, 0:1], 0.25 / S_H, scale3[:, 2:3],
                                                   ALU.mult, ALU.mult).then_inc(thr_made, 1)

            def tile_stats(i, g, which, src):
                for s in range(TILES):
                    nc.vector.bn_stats(stats[:, which, s], src[:, s]).then_inc(ln_stats[which], 1)

            def mean_var(i, g, which):
                for s in range(TILES):
                    nc.vector.bn_aggr(mv[:, which, s], stats[:, which, s]).then_inc(ln_mv[which], 1)
                dve.wait_ge(ln_mv[which], TILES * upto(i, g))
                nc.vector.tensor_scalar(var_s[:, which], mv[:, which, :, 1], LN_EPS, S_N ** -2, ALU.add, ALU.mult)\
                  .then_inc(ln_var[which], 1)

            def normalise(i, g, which, src, dst):
                dve.wait_ge(ln_rstd[which], upto(i, g))
                for s in range(TILES):
                    nc.vector.tensor_scalar(dst[:, s], src[:, s], mv[:, which, s, 0:1], rstd[:, which, s:s + 1],
                                            ALU.subtract, ALU.mult).then_inc(ln_done[which], 1)

            def step(i, k):
                nxt, pr, at, ff, dn = k + 1, k, k - 1, k - 2, k - 3

                def mask_state(c):
                    dve.wait_ge(kv_summed, CH * (upto(i, at) - 1) + c + 1)
                    nc.vector.tensor_tensor(kv_m[:, c], ps_kv, mask[:], ALU.mult).then_inc(kv_masked, 1)

                def rotate(s):
                    dve.wait_ge(qk_projected, TILES * (upto(i, pr) - 1) + s + 1)
                    if s == 0:
                        dve.wait_ge(rope_loaded[pr % 2], 16 * (i + pr // 2 + 1))
                    heads = ps_qk[:, :].rearrange("p (h f) -> p h f", f=DK)
                    pairs = ps_qk[:, :].rearrange("p (h f u) -> p h f u", f=DK // 2, u=2)
                    nc.vector.tensor_tensor(rot[:, s].rearrange("p (h f) -> p h f", f=DK), heads,
                                            rope[:, pr % 2, s, 0:DK].unsqueeze(1).broadcast_to([P, 2 * H, DK]), ALU.mult)
                    nc.vector.tensor_tensor(neg[:, s].rearrange("p (h f u) -> p h f u", f=DK // 2, u=2), pairs[:, :, :, ::-1],
                                            rope[:, pr % 2, s, DK:2 * DK].rearrange("p (f u) -> p f u", u=2).unsqueeze(1)
                                            .broadcast_to([P, 2 * H, DK // 2, 2]), ALU.mult).then_inc(rope_multiplied, 1)

                def negative(s):
                    n = TILES * (upto(i, pr) - 1) + s + 1
                    dve.wait_ge(rope_added, n)
                    nc.vector.tensor_scalar(neg[:, s], rot[:, s], 0.0, None, ALU.min).then_inc(neg_made, 1)

                def elu_one(s):
                    n = TILES * (upto(i, pr) - 1) + s + 1
                    dve.wait_ge(exp_made, n)
                    nc.vector.scalar_tensor_tensor(qk[:, pr % 2, s], rot[:, s], 0.0, neg[:, s], ALU.max, ALU.add)\
                      .then_inc(qk_made, 1)

                def silu_gate(f, p):
                    n = PAIRS * (upto(i, f) - 1) + p + 1
                    dve.wait_ge(gate_up_made, n)
                    dve.wait_ge(tanh_made, n)
                    nc.vector.scalar_tensor_tensor(hid[:, p], hid[:, p], 1.0, ps_gate[p % 2], ALU.add, ALU.mult)\
                      .then_inc(hid_part, 1)
                    dve.wait_ge(hid_part, n)
                    nc.vector.scalar_tensor_tensor(hid[:, p], hid[:, p], S_H / S_N ** 2, ps_up[p % 2], ALU.mult, ALU.mult)\
                      .then_inc(hid_made, 1)

                def gate_num(s):
                    n = TILES * (upto(i, at) - 1) + s + 1
                    dve.wait_ge(num_made, n)
                    nc.vector.tensor_scalar(den[:, s].rearrange("p (h e) -> p h e", h=2), ps_num[s][:, :, P:VW],
                                            DEN_EPS, None, ALU.add).then_inc(den_made, 1)
                    nc.vector.scalar_tensor_tensor(gated[:, s].rearrange("p (h e) -> p h e", h=2),
                                                   gate_t[:, at % 2, s].rearrange("p (h e) -> p h e", h=2), 1.0,
                                                   ps_num[s][:, :, 0:P], ALU.add, ALU.mult)
                    dve.wait_ge(den_made, n)
                    nc.vector.reciprocal(rden[:, s], den[:, s]).then_inc(num_gated, 1)

                if on(i, dn):
                    silu_gate(dn, PAIRS - 1)
                if on(i, at):
                    mask_state(0)
                if k == 1:
                    setup("sums")
                if on(i, ff):
                    normalise(i, ff, 1, x1[:, ff % 2], n2)
                if on(i, pr):
                    rotate(0)
                if k == 0:
                    weights_low(1, 1)
                if k == 1:
                    setup("scales")
                if on(i, at):
                    mask_state(1)
                if on(i, pr):
                    negative(0)
                if k == 1:
                    less(0)
                if on(i, at):
                    mask_state(2)
                if on(i, pr):
                    elu_one(0)
                if k == 0:
                    setup("gate rows")
                if on(i, nxt) and k != 0:
                    dve.wait_ge(x_loaded[nxt % 2], 16 * (i + nxt // 2 + 1))
                    tile_stats(i, nxt, 0, x_in[:, nxt % 2])
                    dve.wait_ge(ln_stats[0], TILES * upto(i, nxt))
                if on(i, at):
                    mask_state(3)
                if on(i, pr):
                    rotate(1)
                if k == 0:
                    setup("gate rows sign")
                if k == 1:
                    ternary(0)
                    setup("output bias")
                if on(i, nxt) and k != 0:
                    mean_var(i, nxt, 0)
                if on(i, ff):
                    dve.wait_ge(h2_hi_made, upto(i, ff))
                    nc.vector.tensor_tensor(h2_lo[:], h2[:], h2_hi[:], ALU.subtract).then_inc(h2_lo_made, 1)
                if on(i, dn):
                    dve.wait_ge(y2_made, upto(i, dn))
                    need(dve, out_made, upto(i, dn) - 1)
                    nc.vector.tensor_tensor(y2g[:], ps_y2, gb_scaled[:, dn % 2:dn % 2 + 1].broadcast_to([P, TILES, D]),
                                            ALU.mult).then_inc(y2_gated, 1)
                if on(i, at):
                    gate_num(0)
                if on(i, pr):
                    negative(1)
                if k == 0:
                    setup("second columns")
                if on(i, at):
                    gate_num(1)
                if k == -1:
                    setup("normalised")
                if on(i, nxt) and k != 0:
                    normalise(i, nxt, 0, x_in[:, nxt % 2], n1)
                if on(i, ff):
                    silu_gate(ff, 0)
                if on(i, pr):
                    elu_one(1)
                if k == 1:
                    setup("output bias low")
                    less(1)
                if k == 2:
                    less(2)
                if on(i, ff):
                    silu_gate(ff, 1)
                if on(i, at):
                    dve.wait_ge(o_hi_made, upto(i, at))
                    nc.vector.tensor_tensor(o_lo[:], ps_tr, o_hi[:], ALU.subtract).then_inc(o_lo_made, 1)
                if k == 1:
                    ternary(1)
                if on(i, ff):
                    silu_gate(ff, 2)
                if on(i, at):
                    dve.wait_ge(y_made, upto(i, at))
                    dve.wait_ge(xr_loaded[at % 2], 16 * (i + at // 2 + 1))
                    need(dve, out_made, upto(i, at) - 2)
                    nc.vector.scalar_tensor_tensor(x1[:, at % 2], ps_y, 1.0 / S_Y, x_res[:, at % 2], ALU.mult, ALU.add)\
                      .then_inc(x1_made, 1)
                    dve.wait_ge(x1_made, upto(i, at))
                    tile_stats(i, at, 1, x1[:, at % 2])
                    dve.wait_ge(ln_stats[1], TILES * upto(i, at))
                if on(i, nxt):
                    dve.wait_ge(n1_hi_made, upto(i, nxt))
                    nc.vector.tensor_tensor(n1_lo[:], ps_tr, n1_hi[:], ALU.subtract).then_inc(n1_lo_made, 1)
                if k == -1:
                    setup("norm split")
                    dve.wait_ge(x_loaded[1], 16)
                    tile_stats(i, 1, 0, x_in[:, 1])
                    dve.wait_ge(ln_stats[0], 2 * TILES)
                    mean_var(i, 1, 0)
                    setup("bias")
                    normalise(i, 1, 0, x_in[:, 1], n1)
                if k == 2:
                    ternary(2)
                if on(i, at):
                    mean_var(i, at, 1)

            steps(dve, step)

        @block.tensor
        def _(pe):
            def mod_columns(kinds):
                for c in range(DC):
                    for n, which in kinds:
                        for kk in range(DC):
                            col = which * D + c * P
                            last = nc.tensor.matmul(ps_mod[:, c, :, n], wmod[:, kk, col:col + P], silu_c[:, kk],
                                                    start=kk == 0, stop=kk == DC - 1)
                last.then_inc(mod_cols, 1)

            def setup(place):
                if place == "norm made":
                    pe.wait_ge(s_wmod_a, 16)
                    pe.wait_ge(silu_made, 1)
                    mod_columns(((0, 0), (1, 1)))
                if place == "norm turned":
                    pe.wait_ge(sa_made, B)
                    pe.wait_ge(s_wa, 16)
                    pe.wait_ge(s_ba, 16)
                    pe.wait_ge(const_made, 5)
                    for half in range(2):
                        cols = slice(512 * half, 512 * (half + 1))
                        for c in range(DC):
                            nc.tensor.matmul(bank[half][:], sa_rows[:, c].rearrange("p a b n -> p (a b n)"),
                                             wa32[:, c, cols], start=c == 0, stop=False)
                        nc.tensor.matmul(bank[half][:], ones[:], ba[:, cols], start=False, stop=True).then_inc(bias_sum, 1)
                    pe.wait_ge(picks_made, 4 * B)
                if place == "first projected":
                    pe.wait_ge(s_wmod_b, 16)
                    for kk in range(DC):
                        rhs = wmod[:, kk].rearrange("p (n d) -> p n d", n=6)[:, 2::3, :]
                        last = nc.tensor.matmul(bank[3][0:B, :].rearrange("p (n d) -> p n d", n=2), silu_c[:, kk], rhs,
                                                start=kk == 0, stop=kk == DC - 1)
                    last.then_inc(gate_rows, 1)
                if place == "first values":
                    pe.wait_ge(shift_made, 1)
                    mod_columns(((2, 3), (3, 4)))
                if place == "gates":
                    pe.wait_ge(gates_made, 1)
                    pe.wait_ge(s_batch, 16)
                    for b in range(B):
                        nc.tensor.matmul(ps_gates[b][:], batch_rows[:, b], gates[:], start=True, stop=True).then_inc(gates_spread, 1)
                if place == "mean":
                    pe.wait_ge(abs_added, 1)
                    nc.tensor.matmul(bank[0][:, 0:3], mean_mat[:], scale3[:], start=True, stop=True).then_inc(scale_sum, 1)
                if place == "before output":
                    pe.wait_ge(wo_lo_made, B)
                    pe.wait_ge(bo_lo_made, 2)
                if place == "before up":
                    pe.wait_ge(ternary_made, 2)
                    pe.wait_ge(gb_made, B)
                if place == "before down":
                    pe.wait_ge(ternary_made, 3)

            pe.wait_ge(const_made, 2)
            for _ in range(WARM_UP):
                nc.tensor.matmul(bank[6][:, 0:P], mean_mat[:], mean_mat[:], start=True, stop=True)

            def turn(src):
                for s in range(TILES):
                    for c in range(DC):
                        last = nc.tensor.transpose(ps_tr[:, c, s * P:(s + 1) * P], src[:, s, c * P:(c + 1) * P], ident[:])
                return last

            def step(i, k):
                nxt, pr, at, ff, dn = k + 1, k, k - 1, k - 2, k - 3

                def project(s, cols, dst, b, sig, first):
                    toks = slice(s * P, (s + 1) * P)
                    if first:
                        pe.wait_ge(wa_lo_made, DC * (b + 1))
                    for c in range(DC):
                        nc.tensor.matmul(dst[:], n1_hi[:, c, toks], wa_hi[:, b, c, cols], start=c == 0, stop=False)
                        nc.tensor.matmul(dst[:], n1_hi[:, c, toks], wa_lo[:, b, c, cols], start=False, stop=False)
                        nc.tensor.matmul(dst[:], n1_lo[:, c, toks], wa_hi[:, b, c, cols], start=False, stop=False)
                    if first:
                        pe.wait_ge(bias_lo, 2)
                    nc.tensor.matmul(dst[:], pick_a[:, b], bias_a[:, cols], start=False, stop=True).then_inc(sig, 1)

                def project_qk(s):
                    if s == 0:
                        need(pe, x1_made, upto(i, pr - 2))
                        pe.wait_ge(n1_lo_made, upto(i, pr))
                    else:
                        pe.wait_ge(rope_multiplied, TILES * (upto(i, pr) - 1) + 1)
                    project(s, slice(0, 2 * D), ps_qk, pr % 2, qk_projected, s == 0 and k in (0, 1))

                def project_vg(s):
                    if s == 0:
                        if k < 3:
                            need(pe, gate_made, TILES * upto(i, pr - 1))
                        else:
                            need(pe, y2_gated, upto(i, dn))
                    else:
                        pe.wait_ge(gate_made, TILES * (upto(i, pr) - 1) + 1)
                    project(s, slice(2 * D, 4 * D), ps_vg, pr % 2, vg_projected, False)

                def sum_kv(c):
                    s, r = c // 2, slice(CS * (c % 2), CS * (c % 2 + 1))
                    if c == 0:
                        need(pe, num_gated, TILES * (upto(i, at) - 1) - 1)
                        if k == 1:
                            pe.wait_ge(second_made, 2)
                        pe.wait_ge(v_copied, TILES * upto(i, at))
                    else:
                        pe.wait_ge(kv_masked, CH * (upto(i, at) - 1) + c)
                    for h in range(2):
                        last = nc.tensor.matmul(ps_kv[:, h], qk[r, at % 2, s, D + h * P:D + (h + 1) * P],
                                                v_ext[r, at % 2, s, h], start=c == 0 and h == 0, stop=c == CH - 1,
                                                skip_group_check=True)
                    last.then_inc(kv_summed, 1)

                def numerator(s):
                    if s == 0:
                        pe.wait_ge(q_copied, upto(i, at))
                        pe.wait_ge(kv_masked, CH * upto(i, at))
                    else:
                        need(pe, rope_multiplied, TILES * upto(i, pr))
                    pe.wait_ge(state_made, CH * (upto(i, at) - 1) + 2 * s + 2)
                    for c in (2 * s, 2 * s + 1):
                        r = CS * (c % 2)
                        for h in range(2):
                            last = nc.tensor.matmul(ps_num[s][r:r + CS, h], q_t[:, h, c * CS:(c + 1) * CS],
                                                    state[:, at % 2, c, h], start=True, stop=True)
                    last.then_inc(num_made, 1)

                def up_gate(p):
                    n = PAIRS * (upto(i, ff) - 1) + p + 1
                    if p == 0:
                        pe.wait_ge(h2_lo_made, upto(i, ff))
                    need(pe, hid_made, n - 2)
                    for dst, w, sig in ((ps_up[p % 2], w_up3, up_made), (ps_gate[p % 2], w_gate3, gate_up_made)):
                        for e in range(2):
                            ee = slice((2 * p + e) * P, (2 * p + e + 1) * P)
                            for c in range(DC):
                                nc.tensor.matmul(dst[:, e], w[:, c, ee], h2_hi[:, c], start=c == 0, stop=False)
                                last = nc.tensor.matmul(dst[:, e], w[:, c, ee], h2_lo[:, c], start=False, stop=c == DC - 1)
                        last.then_inc(sig, 1)

                def down(s):
                    if s == 0:
                        pe.wait_ge(hid_lo_made, PAIRS * upto(i, dn) - 1)
                        need(pe, gate_made, TILES * upto(i, pr - 1))
                    toks = slice(s * P, (s + 1) * P)
                    for e in range(EC):
                        if s == 0 and e == EC - 2:
                            pe.wait_ge(hid_lo_made, PAIRS * upto(i, dn))
                        nc.tensor.matmul(ps_y2[:, s], hid_hi[:, dn % 2, e, toks], w_down3[:, e], start=e == 0, stop=False)
                        last = nc.tensor.matmul(ps_y2[:, s], hid_lo[:, dn % 2, e, toks], w_down3[:, e],
                                                start=False, stop=e == EC - 1)
                    if s == TILES - 1:
                        last.then_inc(y2_made, 1)

                if on(i, at):
                    pe.wait_ge(qk_made, TILES * upto(i, at))
                    need(pe, n1_lo_made, upto(i, pr))
                    turn(qk[:, at % 2]).then_inc(q_turned, 1)
                    sum_kv(0)
                if on(i, pr):
                    project_qk(0)
                if k == 0:
                    setup("first projected")
                if k == 1:
                    setup("mean")
                if k == 3:
                    setup("before down")
                if on(i, at):
                    sum_kv(1)
                if on(i, dn):
                    down(0)
                elif k in (0, 1, 2):
                    project_vg(0)
                if k == 0:
                    setup("first values")
                if on(i, at):
                    sum_kv(2)
                if on(i, pr):
                    project_qk(1)
                if on(i, at):
                    sum_kv(3)
                if on(i, ff):
                    pe.wait_ge(ln_done[1], TILES * upto(i, ff))
                    need(pe, q_copied, upto(i, at))
                    turn(n2).then_inc(n2_turned, 1)
                if on(i, dn):
                    down(1)
                elif k in (0, 1, 2):
                    project_vg(1)
                if on(i, at):
                    numerator(0)
                    numerator(1)
                if k == 2:
                    setup("before up")
                if on(i, ff):
                    up_gate(0)
                if on(i, pr) and k >= 3:
                    project_vg(0)
                if on(i, ff):
                    up_gate(1)
                if on(i, at):
                    pe.wait_ge(o_made, TILES * upto(i, at))
                    need(pe, h2_made, DC * upto(i, ff))
                    turn(o).then_inc(o_turned, 1)
                if on(i, pr) and k >= 3:
                    project_vg(1)
                if on(i, ff):
                    up_gate(2)
                if k == 1:
                    setup("before output")
                if on(i, at):
                    pe.wait_ge(o_lo_made, upto(i, at))
                    pe.wait_ge(num_gated, TILES * upto(i, at))
                    for s in range(TILES):
                        toks = slice(s * P, (s + 1) * P)
                        for c in range(DC):
                            nc.tensor.matmul(ps_y[:, s], o_hi[:, c, toks], wo_hi[:, at % 2, c], start=c == 0, stop=False)
                            nc.tensor.matmul(ps_y[:, s], o_hi[:, c, toks], wo_lo[:, at % 2, c], start=False, stop=False)
                            nc.tensor.matmul(ps_y[:, s], o_lo[:, c, toks], wo_hi[:, at % 2, c], start=False, stop=False)
                        last = nc.tensor.matmul(ps_y[:, s], pick_o[:, at % 2], bias_o[:], start=False, stop=True)
                    last.then_inc(y_made, 1)
                if k == -1:
                    setup("norm made")
                    pe.wait_ge(s_ident, 16)
                if on(i, nxt):
                    pe.wait_ge(ln_done[0], TILES * upto(i, nxt))
                    need(pe, o_lo_made, upto(i, at))
                    turn(n1).then_inc(n1_turned, 1)
                if k == -1:
                    setup("norm turned")
                if k == 0:
                    setup("gates")
                if on(i, ff):
                    up_gate(3)

            steps(pe, step)


def kernel(**inputs):
    import concourse.bacc as bacc
    from concourse.bass_utils import run_bass_kernel_spmd

    a = {k.replace("L0_", ""): np.asarray(v) for k, v in inputs.items()}
    rope, mask, ident = constants()
    arrays = {
        "x": a["attn_x"],
        "w_attn": np.concatenate([a[f"attn_W{n}"].T for n in "qkvg"], 1),
        "w_out": a["attn_Wo"].T,
        "b_attn": np.concatenate([a[f"attn_b{n}"] for n in "qkvg"])[None],
        "b_out": a["attn_bo"][None],
        "w_up": a["ffn_W_up"].T,
        "w_gate": a["ffn_W_gate"].T,
        "w_down": a["ffn_W_down"].T,
        "c_t": a["c"].T,
        "w_mod": a["wmod"],
        "rope_t": rope.reshape(T // GT, P, TILES * 2 * DK),
        "mask_t": mask,
        "ident_t": ident,
        "batch_t": np.repeat(np.eye(B, dtype=np.float32)[:, :, None], P, 2),
    }
    arrays = {k: np.ascontiguousarray(v) for k, v in arrays.items()}
    nc = bacc.Bacc("TRN2", target_bir_lowering=False, num_devices=1)
    args = [nc.dram_tensor(f"in_{k}", v.shape, F32, kind="ExternalInput").ap() for k, v in arrays.items()]
    out = nc.dram_tensor("block_out", (B, T, D), F32, kind="ExternalOutput").ap()
    block_kernel(nc, *args, out)
    r = run_bass_kernel_spmd(nc, [{f"in_{k}": v for k, v in arrays.items()}], core_ids=[0])
    return r.results[0]["block_out"]
```

```python
import numpy as np
import concourse.bass as bass
from concourse import mybir
from contextlib import ExitStack

F32 = mybir.dt.float32
F16 = mybir.dt.float16
ALU = mybir.AluOpType
ACT = mybir.ActivationFunctionType

P = 128
B, T, D = 2, 2048, 256
H = 16
DK = D // H
CS = 64
E = 1024
DC = D // P
EC = E // P
TILES = 2
GT = TILES * P
CH = GT // CS
GROUPS = B * T // GT
OWN_BIAS = 3
FIRST = 5
ABS_CUTS = 2
WARM_UP = 12
PAIRS = EC // 2
QF = 64
QH = QF // DK
QUADS = D // QF
QW = QF + QH

LN_EPS = 1e-5
Q_EPS = 1e-8
DEN_EPS = 1e-6

S_N = 2.0 ** 5
S_W = 2.0 ** 10
S_O = 2.0 ** 4
S_H = 2.0 ** -7
S_QKVG = S_N * S_W
S_Y = S_O * S_W


def constants():
    inv = np.float32(1.0) / np.power(np.float32(10000.0), np.arange(0, DK, 2, dtype=np.float32) / np.float32(DK))
    ang = np.arange(T, dtype=np.float32)[:, None] * inv[None]
    cos, sin = np.cos(ang), np.sin(ang)
    rope = np.empty((T, 2, DK // 2, 2), np.float32)
    rope[:, 0, :, 0] = cos
    rope[:, 0, :, 1] = cos
    rope[:, 1, :, 0] = -sin
    rope[:, 1, :, 1] = sin
    rope *= np.float32(1.0 / S_QKVG)
    rope = rope.reshape(T // GT, TILES, P, 2 * DK).transpose(0, 2, 1, 3).copy()
    head = np.arange(P) // DK
    mask = np.concatenate([head[:, None] % QH == np.arange(QF)[None, :] // DK, head[:, None] % QH == np.arange(QH)[None, :]], 1)
    mask = np.stack([mask] * 2 * DC, 1).astype(np.float32)
    return rope, mask, np.eye(P, dtype=np.float32)


def block_kernel(nc, x, w_attn, w_out, b_attn, b_out, w_up, w_gate, w_down, c_t, w_mod,
                 rope_t, mask_t, ident_t, batch_t, out):
    ctx = ExitStack()
    with ctx:
        def sb(name, shape, dt=F32):
            return ctx.enter_context(nc.sbuf_tensor(name, shape, dt))

        def sem(name):
            return ctx.enter_context(nc.semaphore(name))

        ident = sb("ident", [P, P])
        mask = sb("mask", [P, 2 * DC, QW])
        c_sb = sb("c_sb", [P, DC, B])
        c_th = sb("c_th", [P, DC, B])
        silu_c = sb("silu_c", [P, DC, B])
        batch_rows = sb("batch_rows", [B, B, P])
        wmod = sb("wmod", [P, DC, 6 * D])
        wa32 = sb("wa32", [P, DC, 4 * D])
        wo32 = sb("wo32", [P, DC, D])
        wf32 = sb("wf32", [P, 3, DC * E])
        ba = sb("ba", [1, 4 * D])
        bo_rows = sb("bo_rows", [P, D])
        ones = sb("ones", [1, P])
        mean_mat = sb("mean_mat", [P, P])
        shift = sb("shift", [P, DC, B, 2])
        sa_rows = sb("sa_rows", [P, DC, 2, B, 32])
        ca_scale = sb("ca_scale", [P, DC, B])
        cb_scale = sb("cb_scale", [P, DC, B])
        sb_shift = sb("sb_shift", [P, DC, B])
        gates = sb("gates", [B, 2 * D])
        half_sign = sb("half_sign", [B, 2 * D])
        gate_abs = sb("gate_abs", [B, 2 * D])
        gb_scaled = sb("gb_scaled", [P, B, D])
        bo_gated = sb("bo_gated", [P, B, D])
        wa_hi = sb("wa_hi", [P, B, DC, 4 * D], F16)
        wa_lo = sb("wa_lo", [P, B, DC, 4 * D], F16)
        wo_hi = sb("wo_hi", [P, B, DC, D], F16)
        wo_lo = sb("wo_lo", [P, B, DC, D], F16)
        bias_a = sb("bias_a", [P, 4 * D], F16)
        pick_a = sb("pick_a", [P, B, P], F16)
        vg_bias = sb("vg_bias", [P, B, 2 * D])
        abs_sums = sb("abs_sums", [P, 3, ABS_CUTS])
        scale3 = sb("scale3", [P, 3])
        thr = sb("thr", [P, 2, 3])
        tanh_scale = sb("tanh_scale", [P, 1])
        prod3 = sb("prod3", [P, 2])
        ga_rows = sb("ga_rows", [P, B, D])
        w3 = sb("w3", [P, 3, DC * E], F16)
        w_up3 = w3[:, 0, :].rearrange("p (c e) -> p c e", c=DC)
        w_gate3 = w3[:, 1, :].rearrange("p (c e) -> p c e", c=DC)
        w_down3 = w3[:, 2, :].rearrange("p (e d) -> p e d", e=EC)
        below_down = sb("below_down", [P, DC * E], F16)
        minus_half = sb("minus_half", [P, TILES])

        x_in = sb("x_in", [P, 2, TILES, D])
        x_res = sb("x_res", [P, 2, TILES, D])
        rope = sb("rope", [P, 2, TILES, 2 * DK])
        stats = sb("stats", [P, 2, TILES, 6])
        mv = sb("mv", [P, 2, TILES, 2])
        var_s = sb("var_s", [P, 2, TILES])
        rstd = sb("rstd", [P, 2, TILES])
        n1 = sb("n1", [P, TILES, D])
        n1_hi = sb("n1_hi", [P, DC, GT], F16)
        n1_lo = sb("n1_lo", [P, DC, GT], F16)
        rot = sb("rot", [P, TILES, 2 * D])
        neg = sb("neg", [P, TILES, 2 * D])
        qk = sb("qk", [P, 2, TILES, 2 * D])
        v_ext = sb("v_ext", [P, 2, TILES, QUADS, QW])
        gate_t = sb("gate_t", [P, 2, TILES, D])
        gate_sum = sb("gate_sum", [P, TILES, D])
        q_t = sb("q_t", [P, DC, GT])
        kv_m = sb("kv_m", [P, 2, TILES * DC, QW])
        state = sb("state", [P, B, CH, DC, QW])
        den = sb("den", [P, TILES, H])
        rden = sb("rden", [P, TILES, H])
        gated = sb("gated", [P, TILES, D])
        o = sb("o", [P, TILES, D])
        o_hi = sb("o_hi", [P, DC, GT], F16)
        o_lo = sb("o_lo", [P, DC, GT], F16)
        x1 = sb("x1", [P, 2, TILES, D])
        n2 = sb("n2", [P, TILES, D])
        h2 = sb("h2", [P, DC, GT])
        h2_hi = sb("h2_hi", [P, DC, GT], F16)
        h2_lo = sb("h2_lo", [P, DC, GT], F16)
        hid = sb("hid", [P, PAIRS, 2, GT])
        hid_hi = sb("hid_hi", [P, 2, EC, GT], F16)
        hid_lo = sb("hid_lo", [P, 2, EC, GT], F16)
        y2g = sb("y2g", [P, TILES, D])
        out_sb = sb("out_sb", [P, 2, TILES, D])

        wa_scaled = out_sb[:].rearrange("p a s d -> p a (s d)"), hid[:, 2:4].rearrange("p a b c -> p a (b c)")
        wo_scaled = [x1[:, b] for b in range(B)]
        below = [hid_hi[:, 1].rearrange("p e t -> p (e t)"), hid_lo[:, 1].rearrange("p e t -> p (e t)"), below_down[:]]
        abs_junk = hid[:, 0:2].rearrange("p a b c -> p (a b c)")

        bank = [ctx.enter_context(nc.psum_tensor(f"bank{i}", [P, 512], F32)) for i in range(8)]
        ps_up = [bank[0][:, :].rearrange("p (e t) -> p e t", e=2), bank[2][:, :].rearrange("p (e t) -> p e t", e=2)]
        ps_gate = [bank[1][:, :].rearrange("p (e t) -> p e t", e=2), bank[3][:, :].rearrange("p (e t) -> p e t", e=2)]
        ps_tr = bank[4][:, :].rearrange("p (c t) -> p c t", c=DC)
        ps_qk = bank[5]
        ps_vg = bank[6]
        ps_kv = [bank[b][:, 0:TILES * DC * QW].rearrange("p (h v) -> p h v", v=QW) for b in (7, 1)]
        ps_num = [bank[b][:, 0:TILES * DC * QW].rearrange("p (h v) -> p h v", v=QW) for b in (7, 3)]
        ps_y = bank[5][:, :].rearrange("p (s d) -> p s d", s=TILES)
        ps_mod = [bank[b][:, 0:2 * DC * B].rearrange("p (c b n) -> p c b n", c=DC, b=B) for b in (7, 2)]
        ps_gates = [bank[2], bank[3]]
        ps_y2_last = [bank[7][:, 0:D], bank[5][:, 0:D]]
        ps_y2 = bank[6][:, :].rearrange("p (s d) -> p s d", s=TILES)

        s_c, s_ident, s_ba, s_mask, s_batch, s_wmod_a, s_wmod_b, s_wa, s_wo = [
            sem(f"{n}_loaded") for n in ("c", "ident", "b_attn", "mask", "batch_rows", "wmod_a", "wmod_b", "w_attn", "w_out")]
        s_wf = [sem(f"w_ffn{m}_loaded") for m in range(3)]
        x_loaded = [sem(f"x_loaded{i}") for i in range(2)]
        xr_loaded = [sem(f"xr_loaded{i}") for i in range(2)]
        rope_loaded = [sem(f"rope_loaded{i}") for i in range(2)]
        stored = [sem(f"stored{i}") for i in range(2)]
        c_tanh, silu_made = sem("c_tanh"), sem("silu_made")
        mod_cols, gate_rows, shift_made, sa_made = sem("mod_cols"), sem("gate_rows"), sem("shift_made"), sem("sa_made")
        ca_made, second_made, gates_spread = sem("ca_made"), sem("second_made"), sem("gates_spread")
        half_sign_made, gate_abs_made, gates_made = sem("half_sign_made"), sem("gate_abs_made"), sem("gates_made")
        bias_sum, bias_hi, bias_lo = sem("bias_sum"), sem("bias_hi"), sem("bias_lo")
        wa_scaled_made, wa1_lo_made = sem("wa_scaled_made"), sem("wa1_lo_made")
        wa_hi_made, wa_lo_made, wo_scl, wo_hi_made, wo_lo_made = [
            sem(n) for n in ("wa_hi_made", "wa_lo_made", "wo_scl", "wo_hi_made", "wo_lo_made")]
        bo_gated_made, residual_biased = sem("bo_gated_made"), sem("residual_biased")
        abs_made, abs_added, scale_sum, scale_made, thr_made = [
            sem(n) for n in ("abs_made", "abs_added", "scale_sum", "scale_made", "thr_made")]
        signs_made, below_signs_made = sem("signs_made"), sem("below_signs_made")
        below_made, ternary_made, gb_made = sem("below_made"), sem("ternary_made"), sem("gb_made")
        const_made, ga_spread = sem("const_made"), sem("ga_spread")
        picks_zeroed, picks_made = sem("picks_zeroed"), sem("picks_made")
        ln_stats = [sem(f"ln{i}_stats") for i in (1, 2)]
        ln_mv = [sem(f"ln{i}_mean_var") for i in (1, 2)]
        ln_var = [sem(f"ln{i}_var_scaled") for i in (1, 2)]
        ln_rstd = [sem(f"ln{i}_rstd") for i in (1, 2)]
        ln_done = [sem(f"ln{i}_normalised") for i in (1, 2)]
        n1_turned, n1_hi_made, n1_lo_made = sem("n1_turned"), sem("n1_hi_made"), sem("n1_lo_made")
        qk_projected, vg_projected = sem("qk_projected"), sem("vg_projected")
        rope_multiplied, rope_added, neg_made, exp_made, qk_made = [
            sem(n) for n in ("rope_multiplied", "rope_added", "neg_made", "exp_made", "qk_made")]
        bias_spread, vg_bias_made, gate_biased = sem("bias_spread"), sem("vg_bias_made"), sem("gate_biased")
        v_copied, gate_made = sem("v_copied"), sem("gate_made")
        q_turned, q_copied = sem("q_turned"), sem("q_copied")
        kv_summed, kv_masked, state_made = sem("kv_summed"), sem("kv_masked"), sem("state_made")
        num_made, den_made, rden_made, num_gated, o_made = [
            sem(n) for n in ("num_made", "den_made", "rden_made", "num_gated", "o_made")]
        o_turned, o_hi_made, o_lo_made = sem("o_turned"), sem("o_hi_made"), sem("o_lo_made")
        y_made, x1_made = sem("y_made"), sem("x1_made")
        n2_turned, h2_made, h2_hi_made, h2_lo_made = [sem(n) for n in ("n2_turned", "h2_made", "h2_hi_made", "h2_lo_made")]
        up_made, gate_up_made, tanh_made, hid_part, hid_made, hid_hi_made, hid_lo_made = [
            sem(n) for n in ("up_made", "gate_up_made", "tanh_made", "hid_part", "hid_made", "hid_hi_made", "hid_lo_made")]
        last_hid_lo_made, last_y2_made, last_y2_gated, last_out_made = [
            sem(n) for n in ("last_hid_lo_made", "last_y2_made", "last_y2_gated", "last_out_made")]
        y2_made, y2_gated, out_made = sem("y2_made"), sem("y2_gated"), sem("out_made")

        LAST = GROUPS - 1

        def h2_parts(g):
            return (n1_hi, n1_lo) if g == LAST else (h2_hi, h2_lo)

        block = ctx.enter_context(nc.Block())

        x_v = x.rearrange("b (g s p) d -> b g p s d", s=TILES, p=P)
        out_v = out.rearrange("b (g s p) d -> b g p s d", s=TILES, p=P)

        def need(eng, semaphore, value):
            if not isinstance(value, int) or value > 0:
                eng.wait_ge(semaphore, value)

        def on(i, g):
            return not isinstance(i, int) or 0 <= g < GROUPS

        def upto(i, g):
            return 2 * i + g + 1 if not isinstance(i, int) else max(0, min(g + 1, GROUPS))

        def steps(eng, step):
            for t in range(-1, FIRST):
                step(0, t)
            with eng.Fori(0, (GROUPS - 1 - FIRST) // 2) as i:
                step(i, FIRST)
                step(i, FIRST + 1)
            step(0, GROUPS - 1)
            step(0, GROUPS)

        @block.sync
        def _(sp):
            def load_x(i, g):
                need(sp, ln_done[0], TILES * upto(i, g - 2))
                sp.dma_start(x_in[:, g % 2], x_v[g % 2, i + g // 2]).then_inc(x_loaded[g % 2], 16)

            def load_rope(i, g):
                need(sp, rope_multiplied, TILES * upto(i, g - 2))
                sp.dma_start(rope[:, g % 2], rope_t[i + g // 2].rearrange("p (s c) -> p s c", s=TILES))\
                  .then_inc(rope_loaded[g % 2], 16)

            sp.dma_start(c_sb[:], c_t.rearrange("(k p) b -> p k b", p=P)).then_inc(s_c, 16)
            wmod_v = w_mod.rearrange("(k p) n -> p k n", p=P)
            sp.dma_start(wmod[:, :, 0:2 * D], wmod_v[:, :, 0:2 * D]).then_inc(s_wmod_a, 16)
            load_x(0, 0)
            sp.dma_start(ident[:], ident_t).then_inc(s_ident, 16)
            sp.dma_start(wa32[:], w_attn.rearrange("(c p) n -> p c n", p=P)).then_inc(s_wa, 16)
            sp.dma_start(ba[:], b_attn).then_inc(s_ba, 16)
            load_rope(0, 0)
            sp.dma_start(wmod[:, :, 2 * D:6 * D], wmod_v[:, :, 2 * D:6 * D]).then_inc(s_wmod_b, 16)
            load_x(0, 1)
            sp.dma_start(mask[:], mask_t).then_inc(s_mask, 16)
            sp.dma_start(batch_rows[:], batch_t).then_inc(s_batch, 16)
            sp.dma_start(wo32[:], w_out.rearrange("(c p) n -> p c n", p=P)).then_inc(s_wo, 16)
            sp.dma_start(bo_rows[:], b_out.broadcast_to([P, D])).then_inc(s_wo, 16)
            sp.dma_start(wf32[:, 0].rearrange("p (c e) -> p c e", c=DC), w_up.rearrange("(c p) e -> p c e", p=P)).then_inc(s_wf[0], 16)
            sp.dma_start(wf32[:, 1].rearrange("p (c e) -> p c e", c=DC), w_gate.rearrange("(c p) e -> p c e", p=P)).then_inc(s_wf[1], 16)
            sp.dma_start(wf32[:, 2].rearrange("p (e d) -> p e d", e=EC), w_down.rearrange("(e p) d -> p e d", p=P)).then_inc(s_wf[2], 16)

            def step(i, k):
                if on(i, k + 1) and k >= 1:
                    load_x(i, k + 1)
                if on(i, k + 1) and k >= 0:
                    load_rope(i, k + 1)
                if on(i, k):
                    need(sp, x1_made, upto(i, k - 2))
                    sp.dma_start(x_res[:, k % 2], x_v[k % 2, i + k // 2]).then_inc(xr_loaded[k % 2], 16)
                if on(i, k - 3):
                    d = k - 3
                    sp.wait_ge(out_made, upto(i, d))
                    sp.dma_start(out_v[d % 2, i + d // 2], out_sb[:, d % 2]).then_inc(stored[d % 2], 16)

            steps(sp, step)
            sp.wait_ge(out_made, LAST)
            sp.dma_start(out_v[0, LAST // 2], out_sb[:, 0]).then_inc(stored[0], 16)
            for s in range(TILES):
                sp.wait_ge(last_out_made, s + 1)
                sp.dma_start(out_v[1, LAST // 2, :, s], out_sb[:, 1, s]).then_inc(stored[1], 16)
            sp.wait_ge(stored[0], 16 * (GROUPS // 2))
            sp.wait_ge(stored[1], 16 * (GROUPS // 2 + TILES - 1))

        @block.gpsimd
        def _(pool):
            nc.gpsimd.memset(ones[:], 1.0).then_inc(const_made, 1)
            nc.gpsimd.memset(mean_mat[:], 1.0 / (D * E)).then_inc(const_made, 1)
            nc.gpsimd.memset(minus_half[:], -0.5).then_inc(const_made, 1)
            nc.gpsimd.memset(pick_a[:], 0.0).then_inc(picks_zeroed, 1)
            nc.gpsimd.memset(state[:, :, CH - 1], 0.0).then_inc(const_made, 1)
            nc.gpsimd.memset(v_ext[:, :, :, :, QF:QW], 1.0).then_inc(const_made, 1)
            pool.wait_ge(picks_zeroed, 1)
            pool.wait_ge(const_made, 5)
            n = 0
            for b in range(B):
                for row in (32 * b, 64 + 32 * b):
                    need(pool, picks_made, n)
                    nc.gpsimd.memset(pick_a[row:row + 1, b, :], S_N).then_inc(picks_made, 1)
                    n += 1
            pool.wait_ge(picks_made, n)

            def inverse_std(i, g, which):
                pool.wait_ge(ln_var[which], upto(i, g))
                nc.gpsimd.tensor_tensor(rstd[:, which], var_s[:, which], minus_half[:], ALU.pow)\
                  .then_inc(ln_rstd[which], 1)

            def weights_low(c):
                pool.wait_ge(wa_hi_made, DC + c + 1)
                pool.wait_ge(wa_scaled_made, c + 1)
                parts = lambda w: w[:, 1, c].rearrange("p (a n) -> p a n", a=2)
                nc.gpsimd.tensor_tensor(parts(wa_lo), wa_scaled[c], parts(wa_hi), ALU.subtract).then_inc(wa1_lo_made, 1)

            def setup(place):
                if place == "output weights":
                    pool.wait_ge(s_wo, 32)
                    for b in range(B):
                        pool.wait_ge(ga_spread, b + 1)
                        nc.gpsimd.tensor_tensor(wo_scaled[b], wo32[:], ga_rows[:, b:b + 1].broadcast_to([P, DC, D]), ALU.mult)\
                          .then_inc(wo_scl, 1)
                if place == "output split":
                    for b in range(B):
                        pool.wait_ge(wo_hi_made, b + 1)
                        nc.gpsimd.tensor_tensor(wo_lo[:, b], wo_scaled[b], wo_hi[:, b], ALU.subtract).then_inc(wo_lo_made, 1)

            def step(i, k):
                nxt, pr, at, ff, dn = k + 1, k, k - 1, k - 2, k - 3

                def add_state(c):
                    pool.wait_ge(kv_masked, 2 * (upto(i, at) - 1) + min(c, 1) + 1)
                    if c > 0:
                        pool.wait_ge(state_made, CH * (upto(i, at) - 1) + c)
                    halves = slice(DC * (c // 2), DC * (c // 2 + 1))
                    nc.gpsimd.tensor_tensor(state[:, at % 2, c], state[:, at % 2, (c - 1) % CH], kv_m[:, c % 2, halves], ALU.add)\
                      .then_inc(state_made, 1)

                def add_rope(s):
                    pool.wait_ge(rope_multiplied, TILES * (upto(i, pr) - 1) + s + 1)
                    nc.gpsimd.tensor_tensor(rot[:, s], rot[:, s], neg[:, s], ALU.add).then_inc(rope_added, 1)

                def split_hidden(f, p):
                    pool.wait_ge(hid_hi_made, PAIRS * (upto(i, f) - 1) + p + 1)
                    nc.gpsimd.tensor_tensor(hid_lo[:, f % 2, 2 * p:2 * p + 2], hid[:, p],
                                            hid_hi[:, f % 2, 2 * p:2 * p + 2], ALU.subtract).then_inc(hid_lo_made, 1)

                def divide(u):
                    pool.wait_ge(num_gated, 2 * (upto(i, at) - 1) + u + 1)
                    by_quad = lambda t: t.rearrange("p s (h u e d) -> p (s h) u e d", h=DC, u=2, e=QH)[:, :, u]
                    inverse = rden[:].rearrange("p s (h u e) -> p (s h) u e", h=DC, u=2)[:, :, u]
                    nc.gpsimd.tensor_tensor(by_quad(o[:]), by_quad(gated[:]),
                                            inverse.unsqueeze(3).broadcast_to([P, TILES * DC, QH, DK]), ALU.mult)\
                      .then_inc(o_made, 1)

                def bias_residual():
                    if k == 1:
                        pool.wait_ge(bo_gated_made, 1)
                    pool.wait_ge(xr_loaded[at % 2], 16 * (i + at // 2 + 1))
                    nc.gpsimd.tensor_tensor(x_res[:, at % 2], x_res[:, at % 2],
                                            bo_gated[:, at % 2:at % 2 + 1].broadcast_to([P, TILES, D]), ALU.add)\
                      .then_inc(residual_biased, 1)

                def add_up(g):
                    pool.wait_ge(y2_gated, upto(i, g))
                    need(pool, stored[g % 2], 16 * (i + g // 2))
                    nc.gpsimd.tensor_tensor(out_sb[:, g % 2], y2g[:], x1[:, g % 2], ALU.add).then_inc(out_made, 1)

                if k == GROUPS:
                    inverse_std(i, ff, 1)
                    add_state(0)
                    add_state(1)
                    add_state(2)
                    add_state(3)
                    divide(0)
                    divide(1)
                    bias_residual()
                    add_up(dn)
                    split_hidden(ff, 0)
                    split_hidden(ff, 1)
                    inverse_std(i, at, 1)
                    split_hidden(ff, 2)
                    split_hidden(ff, 3)
                    for p in range(PAIRS - 1):
                        split_hidden(at, p)
                    add_up(ff)
                    return

                if on(i, dn):
                    split_hidden(dn, PAIRS - 1)
                if on(i, ff):
                    inverse_std(i, ff, 1)
                if k == 0:
                    inverse_std(i, nxt, 0)
                if k == 1:
                    setup("output weights")
                    setup("output split")
                if on(i, pr):
                    add_rope(0)
                if k == 0:
                    weights_low(0)
                if on(i, at):
                    add_state(0)
                    add_state(1)
                if on(i, at):
                    add_state(2)
                    add_state(3)
                if on(i, pr):
                    add_rope(1)
                if k == 0:
                    weights_low(1)
                if on(i, nxt) and k != 0:
                    inverse_std(i, nxt, 0)
                if on(i, dn):
                    add_up(dn)
                if on(i, at):
                    divide(0)
                    divide(1)
                    bias_residual()
                if on(i, ff):
                    split_hidden(ff, 0)
                    split_hidden(ff, 1)
                    split_hidden(ff, 2)

            steps(pool, step)

        @block.scalar
        def _(act):
            act.wait_ge(s_c, 16)
            nc.scalar.activation(c_th[:], c_sb[:], ACT.Tanh, scale=0.5).then_inc(c_tanh, 1)

            def less(m, half):
                cols = slice(DC * E // 2 * half, DC * E // 2 * (half + 1))
                act.wait_ge(thr_made, 4)
                n = 2 * (m - 1) + half + 1
                nc.scalar.activation(below[m][:, cols], wf32[:, m, cols], ACT.Sign, scale=-1.0,
                                     bias=thr[:, 1, m:m + 1]).then_inc(signs_made, 1)
                act.wait_ge(signs_made, n)
                nc.scalar.activation(below[m][:, cols], below[m][:, cols], ACT.Relu).then_inc(below_signs_made, 1)

            def sum_abs(m, cuts=range(ABS_CUTS)):
                act.wait_ge(s_wf[m], 16)
                width = DC * E // ABS_CUTS
                for q in cuts:
                    need(act, abs_made, ABS_CUTS * m + q)
                    nc.scalar.activation(abs_junk[:, 0:width], wf32[:, m, width * q:width * (q + 1)], ACT.Abs,
                                         accum_out=abs_sums[:, m, q:q + 1]).then_inc(abs_made, 1)

            def setup(place):
                if place == "norm turned":
                    act.wait_ge(ca_made, 1)
                    act.wait_ge(s_wa, 16)
                    for c in range(DC):
                        nc.scalar.activation(wa_hi[:, 0, c], wa32[:, c], ACT.Copy, scale=ca_scale[:, c, 0:1])\
                          .then_inc(wa_hi_made, 1)
                    for half in range(2):
                        act.wait_ge(bias_sum, half + 1)
                        nc.scalar.activation(bias_a[:, 512 * half:512 * (half + 1)], bank[half][:], ACT.Copy, scale=S_W)\
                          .then_inc(bias_hi, 1)
                        nc.scalar.activation(wa_hi[:, 1, half], wa32[:, half], ACT.Copy, scale=ca_scale[:, half, 1:2])\
                          .then_inc(wa_hi_made, 1)
                    for c in range(DC):
                        nc.scalar.activation(wa_scaled[c], wa32[:, c].rearrange("p (a n) -> p a n", a=2), ACT.Copy,
                                             scale=ca_scale[:, c, 1:2]).then_inc(wa_scaled_made, 1)
                    sum_abs(0, (0,))
                if place == "first exp":
                    sum_abs(0, (1,))
                    sum_abs(1, (0,))
                if place == "second exp":
                    sum_abs(1, (1,))
                if place == "output weights":
                    for b in range(B):
                        act.wait_ge(gates_spread, b + 1)
                        nc.scalar.activation(ga_rows[:, b], ps_gates[b][:, 0:D], ACT.Copy, scale=0.5 * S_W).then_inc(ga_spread, 1)
                    sum_abs(2)
                if place == "spread bias":
                    for b in range(B):
                        act.wait_ge(bias_spread, b + 1)
                        nc.scalar.activation(vg_bias[:, b, 0:D], bank[b][:, 0:D], ACT.Copy, scale=S_O / S_QKVG)
                        nc.scalar.activation(vg_bias[:, b, D:2 * D], bank[b][:, D:2 * D], ACT.Copy).then_inc(vg_bias_made, 1)
                if place == "output split":
                    for b in range(B):
                        act.wait_ge(wo_scl, b + 1)
                        nc.scalar.activation(wo_hi[:, b], wo_scaled[b], ACT.Copy).then_inc(wo_hi_made, 1)
                if place == "down gates":
                    act.wait_ge(thr_made, 5)
                    for b in range(B):
                        nc.scalar.activation(gb_scaled[:, b], ps_gates[b][:, D:2 * D], ACT.Copy, scale=prod3[:, 1:2]).then_inc(gb_made, 1)

            def step(i, k):
                nxt, pr, at, ff, dn = k + 1, k, k - 1, k - 2, k - 3

                def keys_exp(s):
                    act.wait_ge(neg_made, TILES * (upto(i, pr) - 1) + s + 1)
                    nc.scalar.activation(neg[:, s], neg[:, s], ACT.Exp).then_inc(exp_made, 1)

                def values_and_gate(s):
                    n = TILES * (upto(i, pr) - 1) + s + 1
                    act.wait_ge(vg_projected, n)
                    nc.scalar.activation(v_ext[:, pr % 2, s, :, 0:QF],
                                         ps_vg[:, 0:D].rearrange("p (h v) -> p h v", v=QF), ACT.Copy,
                                         scale=S_O / S_QKVG).then_inc(v_copied, 1)
                    nc.scalar.activation(gate_t[:, pr % 2, s], ps_vg[:, D:2 * D], ACT.Tanh,
                                         scale=0.5 / S_QKVG).then_inc(gate_made, 1)

                def gate_tanh(s):
                    act.wait_ge(gate_biased, TILES * (upto(i, pr) - 1) + s + 1 - TILES * OWN_BIAS)
                    nc.scalar.activation(gate_t[:, pr % 2, s], gate_sum[:, s], ACT.Tanh, scale=0.5 / S_QKVG).then_inc(gate_made, 1)

                def tanh_up(f, p):
                    n = PAIRS * (upto(i, f) - 1) + p + 1
                    act.wait_ge(up_made, n)
                    need(act, hid_lo_made, n - PAIRS)
                    nc.scalar.activation(hid[:, p], ps_up[p % 2], ACT.Tanh, scale=tanh_scale[:, 0:1])\
                      .then_inc(tanh_made, 1)

                def hidden_high(f, p):
                    act.wait_ge(hid_made, PAIRS * (upto(i, f) - 1) + p + 1)
                    nc.scalar.activation(hid_hi[:, f % 2, 2 * p:2 * p + 2], hid[:, p], ACT.Copy)\
                      .then_inc(hid_hi_made, 1)

                def modulate(g):
                    act.wait_ge(n2_turned, upto(i, g))
                    for c in range(DC):
                        nc.scalar.activation(h2[:, c], ps_tr[:, c], ACT.Identity,
                                             scale=cb_scale[:, c, g % 2:g % 2 + 1],
                                             bias=sb_shift[:, c, g % 2:g % 2 + 1]).then_inc(h2_made, 1)
                    act.wait_ge(h2_made, DC * upto(i, g))
                    nc.scalar.activation(h2_parts(g)[0][:], h2[:], ACT.Copy).then_inc(h2_hi_made, 1)

                def high_norm():
                    act.wait_ge(n1_turned, upto(i, nxt))
                    nc.scalar.activation(n1_hi[:], ps_tr, ACT.Copy).then_inc(n1_hi_made, 1)

                def output_high():
                    act.wait_ge(o_turned, upto(i, at))
                    nc.scalar.activation(o_hi[:], ps_tr, ACT.Copy).then_inc(o_hi_made, 1)

                if on(i, dn):
                    hidden_high(dn, PAIRS - 1)
                if on(i, at):
                    act.wait_ge(q_turned, upto(i, at))
                    nc.scalar.activation(q_t[:], ps_tr, ACT.Copy).then_inc(q_copied, 1)
                if k == 1:
                    setup("down gates")
                if k == GROUPS:
                    modulate(ff)
                    tanh_up(ff, 0)
                    output_high()
                    hidden_high(ff, 0)
                    tanh_up(ff, 1)
                    hidden_high(ff, 1)
                    tanh_up(ff, 2)
                    hidden_high(ff, 2)
                    tanh_up(ff, 3)
                    modulate(at)
                    hidden_high(ff, 3)
                    tanh_up(at, 0)
                    for p in range(1, PAIRS):
                        tanh_up(at, p)
                        hidden_high(at, p - 1)
                    hidden_high(at, PAIRS - 1)
                    return
                if on(i, ff) and k >= 3:
                    modulate(ff)
                if k in (0, 1, 2):
                    values_and_gate(0)
                if on(i, pr):
                    keys_exp(0)
                if k == 0:
                    setup("first exp")
                    values_and_gate(1)
                if k == 1:
                    less(1, 0)
                    less(1, 1)
                if on(i, ff) and k < 3:
                    modulate(ff)
                if k == 2:
                    less(2, 1)
                if k == 0:
                    high_norm()
                if on(i, pr):
                    keys_exp(1)
                if k == 0:
                    setup("second exp")
                if on(i, ff):
                    tanh_up(ff, 0)
                if on(i, pr) and k != 0:
                    if k < 3:
                        values_and_gate(1)
                if on(i, ff):
                    hidden_high(ff, 0)
                    tanh_up(ff, 1)
                if on(i, at):
                    output_high()
                if k == 1:
                    setup("spread bias")
                    less(2, 0)
                if on(i, ff):
                    hidden_high(ff, 1)
                if on(i, pr) and k >= 3:
                    gate_tanh(0)
                if on(i, ff):
                    tanh_up(ff, 2)
                    hidden_high(ff, 2)
                if on(i, pr) and k >= 3:
                    gate_tanh(1)
                if on(i, nxt) and k != 0:
                    high_norm()
                if k == -1:
                    setup("norm turned")
                if k == 0:
                    setup("output weights")
                    setup("output split")
                if on(i, ff):
                    tanh_up(ff, 3)

            steps(act, step)

        @block.vector
        def _(dve):
            dve.wait_ge(c_tanh, 1)
            nc.vector.scalar_tensor_tensor(silu_c[:], c_th[:], 1.0, c_sb[:], ALU.add, ALU.mult).then_inc(silu_made, 1)

            def weights_low(c):
                dve.wait_ge(wa_hi_made, c + 1)
                nc.vector.scalar_tensor_tensor(wa_lo[:, 0, c], wa32[:, c], ca_scale[:, c, 0:1], wa_hi[:, 0, c],
                                               ALU.mult, ALU.subtract).then_inc(wa_lo_made, 1)

            def less_up():
                dve.wait_ge(thr_made, 4)
                nc.vector.tensor_scalar(below[0], wf32[:, 0], thr[:, 1, 0:1], None, ALU.is_lt).then_inc(below_made, 1)

            def ternary(m, half):
                if m == 0:
                    dve.wait_ge(below_made, 1)
                else:
                    dve.wait_ge(below_signs_made, 2 * (m - 1) + half + 1)
                cols = slice(DC * E // 2 * half, DC * E // 2 * (half + 1))
                nc.vector.scalar_tensor_tensor(w3[:, m, cols], wf32[:, m, cols], thr[:, 0, m:m + 1], below[m][:, cols],
                                               ALU.is_gt, ALU.subtract).then_inc(ternary_made, 1)

            def setup(place):
                if place == "normalised":
                    dve.wait_ge(mod_cols, 1)
                    nc.vector.tensor_scalar(shift[:], ps_mod[0], 0.5, None, ALU.mult).then_inc(shift_made, 1)
                    dve.wait_ge(shift_made, 1)
                    nc.vector.tensor_scalar(ca_scale[:], shift[:, :, :, 1], 1.0, S_W, ALU.add, ALU.mult).then_inc(ca_made, 1)
                    for b in range(B):
                        nc.vector.tensor_copy(sa_rows[:, :, :, b], shift[:, :, b, 0:1].unsqueeze(3)
                                              .broadcast_to([P, DC, 2, 32])).then_inc(sa_made, 1)
                if place == "norm split":
                    dve.wait_ge(ca_made, 1)
                    dve.wait_ge(s_wa, 16)
                    for c in range(DC):
                        weights_low(c)
                if place in ("bias of q, k", "bias of v, gate"):
                    half = 0 if place == "bias of q, k" else 1
                    cols = slice(512 * half, 512 * (half + 1))
                    dve.wait_ge(bias_hi, half + 1)
                    nc.vector.scalar_tensor_tensor(bias_a[64:P, cols], bank[half][64:P, :], S_W, bias_a[64:P, cols],
                                                   ALU.mult, ALU.subtract).then_inc(bias_lo, 1)
                if place == "gate rows":
                    dve.wait_ge(gate_rows, 1)
                    nc.vector.tensor_scalar(half_sign[:], bank[3][0:B, :], 0.0, 0.5, ALU.is_ge, ALU.subtract).then_inc(half_sign_made, 1)
                    dve.wait_ge(half_sign_made, 1)
                    nc.vector.scalar_tensor_tensor(gate_abs[:], half_sign[:], 2.0, bank[3][0:B, :], ALU.mult, ALU.mult)\
                      .then_inc(gate_abs_made, 1)
                if place == "gate rows sign":
                    dve.wait_ge(gate_abs_made, 1)
                    nc.vector.scalar_tensor_tensor(gates[:], gate_abs[:], 0.5, half_sign[:], ALU.max, ALU.mult).then_inc(gates_made, 1)
                if place == "second columns":
                    dve.wait_ge(mod_cols, 2)
                    nc.vector.tensor_scalar(cb_scale[:], ps_mod[1][:, :, :, 1], 0.5, 1.0, ALU.mult, ALU.add).then_inc(second_made, 1)
                    nc.vector.tensor_scalar(sb_shift[:], ps_mod[1][:, :, :, 0], 0.5 * S_N, None, ALU.mult).then_inc(second_made, 1)
                if place == "output bias":
                    dve.wait_ge(ga_spread, B)
                    dve.wait_ge(s_wo, 32)
                    nc.vector.scalar_tensor_tensor(bo_gated[:], bo_rows[:].unsqueeze(1).broadcast_to([P, B, D]), 2.0 / S_W,
                                                   ga_rows[:], ALU.mult, ALU.mult).then_inc(bo_gated_made, 1)
                if place == "sums":
                    dve.wait_ge(abs_made, 3 * ABS_CUTS)
                    nc.vector.tensor_reduce(scale3[:], abs_sums[:], axis=mybir.AxisListType.X, op=ALU.add).then_inc(abs_added, 1)
                    dve.wait_ge(s_mask, 16)
                if place == "scales":
                    dve.wait_ge(scale_sum, 1)
                    nc.vector.tensor_scalar(scale3[:], bank[0][:, 0:3], Q_EPS, None, ALU.add).then_inc(scale_made, 1)
                    dve.wait_ge(scale_made, 1)
                    nc.vector.tensor_scalar(thr[:, 0], scale3[:], 0.5, None, ALU.mult).then_inc(thr_made, 1)
                    nc.vector.tensor_scalar(thr[:, 1], scale3[:], -0.5, None, ALU.mult).then_inc(thr_made, 1)
                    nc.vector.tensor_scalar(tanh_scale[:], scale3[:, 0:1], 0.5 / S_N, None, ALU.mult).then_inc(thr_made, 1)
                    nc.vector.tensor_tensor(prod3[:, 0:1], scale3[:, 0:1], scale3[:, 1:2], ALU.mult).then_inc(thr_made, 1)
                    dve.wait_ge(thr_made, 4)
                    nc.vector.scalar_tensor_tensor(prod3[:, 1:2], prod3[:, 0:1], 0.5 / S_H, scale3[:, 2:3],
                                                   ALU.mult, ALU.mult).then_inc(thr_made, 1)

            def tile_stats(i, g, which, src):
                for s in range(TILES):
                    nc.vector.bn_stats(stats[:, which, s], src[:, s]).then_inc(ln_stats[which], 1)

            def mean_var(i, g, which):
                for s in range(TILES):
                    nc.vector.bn_aggr(mv[:, which, s], stats[:, which, s]).then_inc(ln_mv[which], 1)
                dve.wait_ge(ln_mv[which], TILES * upto(i, g))
                nc.vector.tensor_scalar(var_s[:, which], mv[:, which, :, 1], LN_EPS, S_N ** -2, ALU.add, ALU.mult)\
                  .then_inc(ln_var[which], 1)

            def normalise(i, g, which, src, dst):
                dve.wait_ge(ln_rstd[which], upto(i, g))
                for s in range(TILES):
                    nc.vector.tensor_scalar(dst[:, s], src[:, s], mv[:, which, s, 0:1], rstd[:, which, s:s + 1],
                                            ALU.subtract, ALU.mult).then_inc(ln_done[which], 1)

            def step(i, k):
                nxt, pr, at, ff, dn = k + 1, k, k - 1, k - 2, k - 3

                def mask_state(c):
                    dve.wait_ge(kv_summed, upto(i, at))
                    nc.vector.tensor_tensor(kv_m[:, c], ps_kv[c], mask[:], ALU.mult).then_inc(kv_masked, 1)

                def rotate(s):
                    dve.wait_ge(qk_projected, TILES * (upto(i, pr) - 1) + s + 1)
                    if s == 0:
                        dve.wait_ge(rope_loaded[pr % 2], 16 * (i + pr // 2 + 1))
                    heads = ps_qk[:, :].rearrange("p (h f) -> p h f", f=DK)
                    pairs = ps_qk[:, :].rearrange("p (h f u) -> p h f u", f=DK // 2, u=2)
                    nc.vector.tensor_tensor(rot[:, s].rearrange("p (h f) -> p h f", f=DK), heads,
                                            rope[:, pr % 2, s, 0:DK].unsqueeze(1).broadcast_to([P, 2 * H, DK]), ALU.mult)
                    nc.vector.tensor_tensor(neg[:, s].rearrange("p (h f u) -> p h f u", f=DK // 2, u=2), pairs[:, :, :, ::-1],
                                            rope[:, pr % 2, s, DK:2 * DK].rearrange("p (f u) -> p f u", u=2).unsqueeze(1)
                                            .broadcast_to([P, 2 * H, DK // 2, 2]), ALU.mult).then_inc(rope_multiplied, 1)

                def vg_bias_add(s):
                    dve.wait_ge(vg_projected, TILES * (upto(i, pr) - 1) + s + 1)
                    quads = lambda t: t.rearrange("p (h v) -> p h v", v=QF)
                    nc.vector.scalar_tensor_tensor(v_ext[:, pr % 2, s, :, 0:QF], quads(ps_vg[:, 0:D]), S_O / S_QKVG,
                                                   quads(vg_bias[:, pr % 2, 0:D]), ALU.mult, ALU.add).then_inc(v_copied, 1)
                    nc.vector.tensor_tensor(gate_sum[:, s], ps_vg[:, D:2 * D], vg_bias[:, pr % 2, D:2 * D], ALU.add)\
                      .then_inc(gate_biased, 1)

                def negative(s):
                    n = TILES * (upto(i, pr) - 1) + s + 1
                    dve.wait_ge(rope_added, n)
                    nc.vector.tensor_scalar(neg[:, s], rot[:, s], 0.0, None, ALU.min).then_inc(neg_made, 1)

                def elu_one(s):
                    n = TILES * (upto(i, pr) - 1) + s + 1
                    dve.wait_ge(exp_made, n)
                    nc.vector.scalar_tensor_tensor(qk[:, pr % 2, s], rot[:, s], 0.0, neg[:, s], ALU.max, ALU.add)\
                      .then_inc(qk_made, 1)

                def silu_gate(f, p, before_second=None):
                    n = PAIRS * (upto(i, f) - 1) + p + 1
                    dve.wait_ge(gate_up_made, n)
                    dve.wait_ge(tanh_made, n)
                    nc.vector.scalar_tensor_tensor(hid[:, p], hid[:, p], 1.0, ps_gate[p % 2], ALU.add, ALU.mult)\
                      .then_inc(hid_part, 1)
                    if before_second:
                        dve.wait_ge(*before_second)
                    dve.wait_ge(hid_part, n)
                    nc.vector.scalar_tensor_tensor(hid[:, p], hid[:, p], S_H / S_N ** 2, ps_up[p % 2], ALU.mult, ALU.mult)\
                      .then_inc(hid_made, 1)

                def gate_num(u):
                    n = 2 * (upto(i, at) - 1) + u + 1
                    by_quad = lambda t: t.rearrange("p s (h u e) -> p (s h) u e", h=DC, u=2)[:, :, u]
                    dve.wait_ge(num_made, upto(i, at))
                    if u == 0:
                        dve.wait_ge(gate_made, TILES * upto(i, at))
                    nc.vector.tensor_scalar(by_quad(den[:]), ps_num[u][:, :, QF:QW], DEN_EPS, None, ALU.add).then_inc(den_made, 1)
                    nc.vector.scalar_tensor_tensor(by_quad(gated[:]), by_quad(gate_t[:, at % 2]), 1.0,
                                                   ps_num[u][:, :, 0:QF], ALU.add, ALU.mult)
                    dve.wait_ge(den_made, n)
                    nc.vector.reciprocal(by_quad(rden[:]), by_quad(den[:])).then_inc(num_gated, 1)

                def modulated_low(g):
                    dve.wait_ge(h2_hi_made, upto(i, g))
                    hi, lo = h2_parts(g)
                    nc.vector.tensor_tensor(lo[:], h2[:], hi[:], ALU.subtract).then_inc(h2_lo_made, 1)

                def gate_down(g):
                    dve.wait_ge(y2_made, upto(i, g))
                    need(dve, out_made, upto(i, g) - 1)
                    nc.vector.tensor_tensor(y2g[:], ps_y2, gb_scaled[:, g % 2:g % 2 + 1].broadcast_to([P, TILES, D]),
                                            ALU.mult).then_inc(y2_gated, 1)

                def output_low():
                    dve.wait_ge(o_hi_made, upto(i, at))
                    nc.vector.tensor_tensor(o_lo[:], ps_tr, o_hi[:], ALU.subtract).then_inc(o_lo_made, 1)

                def residual():
                    dve.wait_ge(y_made, upto(i, at))
                    dve.wait_ge(residual_biased, upto(i, at))
                    need(dve, out_made, upto(i, at) - 2)
                    nc.vector.scalar_tensor_tensor(x1[:, at % 2], ps_y, 1.0 / S_Y, x_res[:, at % 2], ALU.mult, ALU.add)\
                      .then_inc(x1_made, 1)
                    dve.wait_ge(x1_made, upto(i, at))
                    nc.vector.bn_stats(stats[:, 1, 0], x1[:, at % 2, 0]).then_inc(ln_stats[1], 1)

                if k == GROUPS:
                    dve.wait_ge(ln_stats[1], TILES * upto(i, ff))
                    silu_gate(dn, PAIRS - 1)
                    mean_var(i, ff, 1)
                    mask_state(0)
                    mask_state(1)
                    normalise(i, ff, 1, x1[:, ff % 2], n2)
                    dve.wait_ge(hid_hi_made, PAIRS * upto(i, dn))
                    nc.vector.tensor_tensor(hid_lo[:, dn % 2, EC - 2:EC], hid[:, PAIRS - 1], hid_hi[:, dn % 2, EC - 2:EC],
                                            ALU.subtract).then_inc(hid_lo_made, 1)
                    modulated_low(ff)
                    gate_num(0)
                    gate_num(1)
                    gate_down(dn)
                    silu_gate(ff, 0)
                    output_low()
                    silu_gate(ff, 1)
                    residual()
                    nc.vector.bn_stats(stats[:, 1, 1], x1[:, at % 2, 1]).then_inc(ln_stats[1], 1)
                    dve.wait_ge(ln_stats[1], TILES * upto(i, at))
                    mean_var(i, at, 1)
                    silu_gate(ff, 2)
                    normalise(i, at, 1, x1[:, at % 2], n2)
                    silu_gate(ff, 3)
                    modulated_low(at)
                    for p in range(PAIRS):
                        silu_gate(at, p)
                    dve.wait_ge(hid_hi_made, PAIRS * GROUPS)
                    nc.vector.tensor_tensor(hid_lo[:, at % 2, EC - 2:EC], hid[:, PAIRS - 1], hid_hi[:, at % 2, EC - 2:EC],
                                            ALU.subtract).then_inc(last_hid_lo_made, 1)
                    gate_down(ff)
                    dve.wait_ge(stored[at % 2], 16 * (GROUPS // 2 - 1))
                    for s in range(TILES):
                        dve.wait_ge(last_y2_made, s + 1)
                        nc.vector.tensor_tensor(out_sb[:, at % 2, s], ps_y2_last[s], gb_scaled[:, at % 2], ALU.mult)\
                          .then_inc(last_y2_gated, 1)
                        dve.wait_ge(last_y2_gated, s + 1)
                        nc.vector.tensor_tensor(out_sb[:, at % 2, s], out_sb[:, at % 2, s], x1[:, at % 2, s], ALU.add)\
                          .then_inc(last_out_made, 1)
                    return

                if on(i, ff) and not on(i, dn):
                    dve.wait_ge(ln_stats[1], TILES * upto(i, ff))
                if on(i, dn):
                    silu_gate(dn, PAIRS - 1, before_second=(ln_stats[1], TILES * upto(i, ff)))
                if on(i, ff):
                    mean_var(i, ff, 1)
                if on(i, at):
                    mask_state(0)
                    mask_state(1)
                if on(i, pr):
                    rotate(0)
                if on(i, ff):
                    normalise(i, ff, 1, x1[:, ff % 2], n2)
                if k == 1:
                    setup("scales")
                    less_up()
                if k == OWN_BIAS - 1:
                    dve.wait_ge(vg_bias_made, B)
                    ternary(1, 1)
                if on(i, pr):
                    negative(0)
                if k == 0:
                    setup("gate rows")
                    elu_one(0)
                if on(i, pr):
                    rotate(1)
                if on(i, nxt) and k != 0:
                    dve.wait_ge(x_loaded[nxt % 2], 16 * (i + nxt // 2 + 1))
                    tile_stats(i, nxt, 0, x_in[:, nxt % 2])
                    dve.wait_ge(ln_stats[0], TILES * upto(i, nxt))
                if on(i, ff):
                    modulated_low(ff)
                if on(i, nxt) and k != 0:
                    mean_var(i, nxt, 0)
                if on(i, pr) and k != 0:
                    elu_one(0)
                if k == 0:
                    setup("gate rows sign")
                if k == 1:
                    ternary(0, 0)
                if on(i, dn):
                    gate_down(dn)
                if on(i, at):
                    gate_num(0)
                if on(i, pr):
                    negative(1)
                if k == 1:
                    setup("second columns")
                if on(i, at):
                    gate_num(1)
                if k == -1:
                    setup("normalised")
                if on(i, nxt) and k != 0:
                    normalise(i, nxt, 0, x_in[:, nxt % 2], n1)
                if on(i, ff):
                    silu_gate(ff, 0)
                if on(i, pr):
                    elu_one(1)
                if on(i, pr) and k >= OWN_BIAS:
                    vg_bias_add(0)
                if on(i, ff):
                    silu_gate(ff, 1)
                if on(i, at):
                    output_low()
                if on(i, pr) and k >= OWN_BIAS:
                    vg_bias_add(1)
                if k == 1:
                    ternary(0, 1)
                if k == 2:
                    ternary(2, 0)
                    ternary(2, 1)
                if on(i, ff):
                    silu_gate(ff, 2)
                if on(i, at):
                    residual()
                if on(i, at) and k >= 3:
                    nc.vector.bn_stats(stats[:, 1, 1], x1[:, at % 2, 1]).then_inc(ln_stats[1], 1)
                if on(i, nxt):
                    dve.wait_ge(n1_hi_made, upto(i, nxt))
                    nc.vector.tensor_tensor(n1_lo[:], ps_tr, n1_hi[:], ALU.subtract).then_inc(n1_lo_made, 1)
                if k == 1:
                    ternary(1, 0)
                if on(i, at) and k < 3:
                    nc.vector.bn_stats(stats[:, 1, 1], x1[:, at % 2, 1]).then_inc(ln_stats[1], 1)
                if k == -1:
                    setup("norm split")
                    setup("bias of q, k")
                    dve.wait_ge(x_loaded[1], 16)
                    tile_stats(i, 1, 0, x_in[:, 1])
                    dve.wait_ge(ln_stats[0], 2 * TILES)
                    mean_var(i, 1, 0)
                    setup("bias of v, gate")
                    normalise(i, 1, 0, x_in[:, 1], n1)
                if k == 0:
                    setup("output bias")
                    setup("sums")

            steps(dve, step)

        @block.tensor
        def _(pe):
            def mod_columns(dst, kinds):
                for c in range(DC):
                    for n, which in enumerate(kinds):
                        for kk in range(DC):
                            col = which * D + c * P
                            last = nc.tensor.matmul(dst[:, c, :, n], wmod[:, kk, col:col + P], silu_c[:, kk],
                                                    start=kk == 0, stop=kk == DC - 1)
                last.then_inc(mod_cols, 1)

            def setup(place):
                if place == "norm made":
                    pe.wait_ge(s_wmod_a, 16)
                    pe.wait_ge(silu_made, 1)
                    mod_columns(ps_mod[0], (0, 1))
                    keep_busy(5)
                if place == "norm turned":
                    pe.wait_ge(sa_made, B)
                    pe.wait_ge(s_wa, 16)
                    pe.wait_ge(s_ba, 16)
                    pe.wait_ge(const_made, 5)
                    for half in range(2):
                        cols = slice(512 * half, 512 * (half + 1))
                        for c in range(DC):
                            nc.tensor.matmul(bank[half][:], sa_rows[:, c].rearrange("p a b n -> p (a b n)"),
                                             wa32[:, c, cols], start=c == 0, stop=False)
                        nc.tensor.matmul(bank[half][:], ones[:], ba[:, cols], start=False, stop=True).then_inc(bias_sum, 1)
                    pe.wait_ge(picks_made, 2 * B)
                if place == "first projected":
                    pe.wait_ge(s_wmod_b, 16)
                    for kk in range(DC):
                        rhs = wmod[:, kk].rearrange("p (n d) -> p n d", n=6)[:, 2::3, :]
                        last = nc.tensor.matmul(bank[3][0:B, :].rearrange("p (n d) -> p n d", n=2), silu_c[:, kk], rhs,
                                                start=kk == 0, stop=kk == DC - 1)
                    last.then_inc(gate_rows, 1)
                if place == "second columns":
                    mod_columns(ps_mod[1], (3, 4))
                if place == "gates":
                    pe.wait_ge(gates_made, 1)
                    pe.wait_ge(s_batch, 16)
                    for b in range(B):
                        nc.tensor.matmul(ps_gates[b][:], batch_rows[:, b], gates[:], start=True, stop=True).then_inc(gates_spread, 1)
                if place == "mean":
                    pe.wait_ge(abs_added, 1)
                    nc.tensor.matmul(bank[0][:, 0:3], mean_mat[:], scale3[:], start=True, stop=True).then_inc(scale_sum, 1)
                if place == "before output":
                    pe.wait_ge(wo_lo_made, B)
                if place == "before up":
                    pe.wait_ge(ternary_made, 4)
                    pe.wait_ge(gb_made, B)
                    pe.wait_ge(second_made, 2)
                if place == "before down":
                    pe.wait_ge(ternary_made, 6)

            def keep_busy(products, free=bank[0]):
                for _ in range(products):
                    nc.tensor.matmul(free[:, 0:P], mean_mat[:], mean_mat[:], start=True, stop=True)

            pe.wait_ge(const_made, 2)
            keep_busy(WARM_UP)

            def turn(src):
                for s in range(TILES):
                    for c in range(DC):
                        last = nc.tensor.transpose(ps_tr[:, c, s * P:(s + 1) * P], src[:, s, c * P:(c + 1) * P], ident[:])
                return last

            def step(i, k):
                nxt, pr, at, ff, dn = k + 1, k, k - 1, k - 2, k - 3

                def project(s, cols, dst, b, sig, first):
                    toks = slice(s * P, (s + 1) * P)
                    with_bias = dst is ps_qk or k < OWN_BIAS
                    if first:
                        pe.wait_ge(wa1_lo_made if b else wa_lo_made, DC)
                    for c in range(DC):
                        nc.tensor.matmul(dst[:], n1_hi[:, c, toks], wa_hi[:, b, c, cols], start=c == 0, stop=False)
                        nc.tensor.matmul(dst[:], n1_hi[:, c, toks], wa_lo[:, b, c, cols], start=False, stop=False)
                        last = nc.tensor.matmul(dst[:], n1_lo[:, c, toks], wa_hi[:, b, c, cols], start=False,
                                                stop=c == DC - 1 and not with_bias)
                    if first:
                        pe.wait_ge(bias_lo, 1)
                    elif k == 0 and s == 0:
                        pe.wait_ge(bias_lo, 2)
                    if with_bias:
                        last = nc.tensor.matmul(dst[:], pick_a[:, b], bias_a[:, cols], start=False, stop=True)
                    last.then_inc(sig, 1)

                def project_qk(s):
                    if s == 0:
                        need(pe, x1_made, upto(i, pr - 2))
                        pe.wait_ge(n1_lo_made, upto(i, pr))
                    else:
                        pe.wait_ge(rope_multiplied, TILES * (upto(i, pr) - 1) + 1)
                    project(s, slice(0, 2 * D), ps_qk, pr % 2, qk_projected, s == 0 and k in (0, 1))

                def vg_is_read(tiles, g):
                    if g < OWN_BIAS:
                        need(pe, gate_made, tiles)
                    else:
                        pe.wait_ge(gate_biased, tiles - TILES * OWN_BIAS)

                def project_vg(s):
                    if s == 0:
                        if k < 3:
                            need(pe, gate_made, TILES * upto(i, pr - 1))
                        else:
                            need(pe, y2_gated, upto(i, dn))
                    else:
                        vg_is_read(TILES * (upto(i, pr) - 1) + 1, k)
                    project(s, slice(2 * D, 4 * D), ps_vg, pr % 2, vg_projected, False)

                def kv_waits(g):
                    need(pe, num_gated, 2 * upto(i, g - 1) - 1)
                    if g == 1:
                        pe.wait_ge(vg_bias_made, B)
                    need(pe, hid_made, PAIRS * upto(i, g - 2) - 1)
                    if g == 0:
                        pe.wait_ge(shift_made, 1)
                    pe.wait_ge(v_copied, TILES * upto(i, g))
                    pe.wait_ge(qk_made, TILES * upto(i, g))

                def numerator_waits():
                    pe.wait_ge(q_copied, upto(i, at))
                    pe.wait_ge(kv_masked, TILES * (upto(i, at) - 1) + 1)
                    need(pe, hid_made, PAIRS * upto(i, at - 2))
                    if k == 1:
                        pe.wait_ge(gb_made, B)
                    pe.wait_ge(state_made, CH * upto(i, at))

                def sum_kv():
                    for s in range(TILES):
                        for h in range(DC):
                            for u in range(2):
                                for c in range(2):
                                    r = slice(CS * c, CS * (c + 1))
                                    f = slice(D + h * P + u * QF, D + h * P + (u + 1) * QF)
                                    last = nc.tensor.matmul(ps_kv[c][QF * u:QF * (u + 1), DC * s + h], qk[r, at % 2, s, f],
                                                            v_ext[r, at % 2, s, 2 * h + u], start=True, stop=True)
                    last.then_inc(kv_summed, 1)

                def numerator():
                    for s in range(TILES):
                        for h in range(DC):
                            for u in range(2):
                                f = slice(QF * u, QF * (u + 1))
                                for c in range(2):
                                    toks = slice((2 * s + c) * CS, (2 * s + c + 1) * CS)
                                    last = nc.tensor.matmul(ps_num[u][CS * c:CS * (c + 1), DC * s + h], q_t[f, h, toks],
                                                            state[f, at % 2, 2 * s + c, h], start=True, stop=True)
                    last.then_inc(num_made, 1)

                def up_gate(f, p):
                    n = PAIRS * (upto(i, f) - 1) + p + 1
                    hi, lo = h2_parts(f)
                    if p == 0:
                        pe.wait_ge(h2_lo_made, upto(i, f))
                        pe.wait_ge(kv_masked, 2 * upto(i, f + 1))
                    if p == 1:
                        pe.wait_ge(num_gated, 2 * upto(i, f + 1))
                    need(pe, hid_made, n - 2)
                    for dst, w, sig in ((ps_up[p % 2], w_up3, up_made), (ps_gate[p % 2], w_gate3, gate_up_made)):
                        for e in range(2):
                            if p == PAIRS - 1 and sig is gate_up_made and e == 1 and f + 2 < GROUPS:
                                kv_waits(f + 2)
                            ee = slice((2 * p + e) * P, (2 * p + e + 1) * P)
                            for c in range(DC):
                                nc.tensor.matmul(dst[:, e], w[:, c, ee], hi[:, c], start=c == 0, stop=False)
                                last = nc.tensor.matmul(dst[:, e], w[:, c, ee], lo[:, c], start=False, stop=c == DC - 1)
                        last.then_inc(sig, 1)

                def down(s):
                    if s == 0:
                        pe.wait_ge(hid_lo_made, PAIRS * upto(i, dn) - 1)
                        vg_is_read(TILES * upto(i, pr - 1), k - 1)
                    toks = slice(s * P, (s + 1) * P)
                    for e in range(EC):
                        if s == 0 and e == EC - 2:
                            pe.wait_ge(hid_lo_made, PAIRS * upto(i, dn))
                        if s == TILES - 1 and e == EC - 1 and on(i, at):
                            numerator_waits()
                        nc.tensor.matmul(ps_y2[:, s], hid_hi[:, dn % 2, e, toks], w_down3[:, e], start=e == 0, stop=False)
                        last = nc.tensor.matmul(ps_y2[:, s], hid_lo[:, dn % 2, e, toks], w_down3[:, e],
                                                start=False, stop=e == EC - 1)
                    if s == TILES - 1:
                        last.then_inc(y2_made, 1)

                def down_pair(g, p):
                    if g == LAST and p == PAIRS - 1:
                        pe.wait_ge(last_hid_lo_made, 1)
                    else:
                        pe.wait_ge(hid_lo_made, PAIRS * g + p + 1)
                    for s in range(TILES):
                        toks = slice(s * P, (s + 1) * P)
                        dst = ps_y2_last[s] if g == LAST else ps_y2[:, s]
                        for e in (2 * p, 2 * p + 1):
                            nc.tensor.matmul(dst, hid_hi[:, g % 2, e, toks], w_down3[:, e],
                                             start=e == 0 and (g == LAST or s == 0), stop=False, skip_group_check=True)
                            last = nc.tensor.matmul(dst, hid_lo[:, g % 2, e, toks], w_down3[:, e],
                                                    start=False, stop=e == EC - 1, skip_group_check=True)
                        if g == LAST and p == PAIRS - 1:
                            last.then_inc(last_y2_made, 1)
                    return last

                def turn_norm(g):
                    pe.wait_ge(ln_done[1], TILES * upto(i, g))
                    turn(n2).then_inc(n2_turned, 1)

                def turn_output():
                    pe.wait_ge(o_made, TILES * upto(i, at))
                    need(pe, h2_made, DC * upto(i, ff))
                    turn(o).then_inc(o_turned, 1)

                def project_output():
                    pe.wait_ge(o_lo_made, upto(i, at))
                    need(pe, rope_multiplied, TILES * upto(i, pr))
                    for s in range(TILES):
                        toks = slice(s * P, (s + 1) * P)
                        for c in range(DC):
                            nc.tensor.matmul(ps_y[:, s], o_hi[:, c, toks], wo_hi[:, at % 2, c], start=c == 0, stop=False)
                            nc.tensor.matmul(ps_y[:, s], o_hi[:, c, toks], wo_lo[:, at % 2, c], start=False, stop=False)
                            last = nc.tensor.matmul(ps_y[:, s], o_lo[:, c, toks], wo_hi[:, at % 2, c],
                                                    start=False, stop=c == DC - 1)
                    last.then_inc(y_made, 1)

                if k == GROUPS:
                    sum_kv()
                    turn(qk[:, at % 2]).then_inc(q_turned, 1)
                    vg_is_read(TILES * GROUPS, LAST)
                    for p in range(PAIRS - 1):
                        down_pair(dn, p)
                    pe.wait_ge(q_copied, upto(i, at))
                    turn_norm(ff)
                    down_pair(dn, PAIRS - 1).then_inc(y2_made, 1)
                    numerator_waits()
                    numerator()
                    up_gate(ff, 0)
                    turn_output()
                    up_gate(ff, 1)
                    project_output()
                    up_gate(ff, 2)
                    up_gate(ff, 3)
                    pe.wait_ge(y2_gated, upto(i, dn))
                    down_pair(ff, 0)
                    pe.wait_ge(o_lo_made, upto(i, at))
                    turn_norm(at)
                    down_pair(ff, 1)
                    down_pair(ff, 2)
                    for p in range(PAIRS):
                        up_gate(at, p)
                    down_pair(ff, PAIRS - 1).then_inc(y2_made, 1)
                    pe.wait_ge(x1_made, upto(i, at))
                    for p in range(PAIRS):
                        down_pair(at, p)
                    return

                if on(i, at):
                    if k < 3:
                        kv_waits(at)
                    sum_kv()
                if on(i, pr):
                    project_qk(0)
                if k == 1:
                    setup("mean")
                if on(i, at):
                    need(pe, n1_lo_made, upto(i, pr))
                    turn(qk[:, at % 2]).then_inc(q_turned, 1)
                if k == 0:
                    setup("first projected")
                if k == 3:
                    setup("before down")
                if on(i, dn):
                    down(0)
                elif k in (0, 1, 2):
                    project_vg(0)
                if on(i, pr):
                    project_qk(1)
                if on(i, ff):
                    need(pe, q_copied, upto(i, at))
                    turn_norm(ff)
                if on(i, dn):
                    down(1)
                elif k in (0, 1, 2):
                    project_vg(1)
                if on(i, at):
                    if not on(i, dn):
                        numerator_waits()
                    numerator()
                if k == 2:
                    setup("before up")
                if on(i, ff):
                    up_gate(ff, 0)
                if on(i, pr) and k >= 3:
                    project_vg(0)
                if on(i, ff):
                    up_gate(ff, 1)
                if k == 1:
                    setup("second columns")
                    pe.wait_ge(scale_made, 1)
                    pe.wait_ge(kv_masked, 2)
                    for b in range(B):
                        nc.tensor.matmul(bank[b][:], pick_a[:, b], bias_a[:, 2 * D:4 * D], start=True, stop=True)\
                          .then_inc(bias_spread, 1)
                    pe.wait_ge(second_made, 2)
                    keep_busy(6, bank[2])
                if on(i, at):
                    turn_output()
                if on(i, ff):
                    up_gate(ff, 2)
                if on(i, pr) and k >= 3:
                    project_vg(1)
                if k == 1:
                    keep_busy(5, bank[2])
                    setup("before output")
                if on(i, at):
                    project_output()
                if k == -1:
                    setup("norm made")
                    pe.wait_ge(s_ident, 16)
                if on(i, nxt):
                    pe.wait_ge(ln_done[0], TILES * upto(i, nxt))
                    need(pe, o_lo_made, upto(i, at))
                    turn(n1).then_inc(n1_turned, 1)
                if k == -1:
                    setup("norm turned")
                if k == 0:
                    pe.wait_ge(bias_lo, 2)
                    keep_busy(6)
                    setup("gates")
                    keep_busy(4)
                if on(i, ff):
                    up_gate(ff, 3)

            steps(pe, step)


def kernel(**inputs):
    import concourse.bacc as bacc
    from concourse.bass_utils import run_bass_kernel_spmd

    a = {k.replace("L0_", ""): np.asarray(v) for k, v in inputs.items()}
    rope, mask, ident = constants()
    arrays = {
        "x": a["attn_x"],
        "w_attn": np.concatenate([a[f"attn_W{n}"].T for n in "qkvg"], 1),
        "w_out": a["attn_Wo"].T,
        "b_attn": np.concatenate([a[f"attn_b{n}"] for n in "qkvg"])[None],
        "b_out": a["attn_bo"][None],
        "w_up": a["ffn_W_up"].T,
        "w_gate": a["ffn_W_gate"].T,
        "w_down": a["ffn_W_down"].T,
        "c_t": a["c"].T,
        "w_mod": a["wmod"],
        "rope_t": rope.reshape(T // GT, P, TILES * 2 * DK),
        "mask_t": mask,
        "ident_t": ident,
        "batch_t": np.repeat(np.eye(B, dtype=np.float32)[:, :, None], P, 2),
    }
    arrays = {k: np.ascontiguousarray(v) for k, v in arrays.items()}
    nc = bacc.Bacc("TRN2", target_bir_lowering=False, num_devices=1)
    args = [nc.dram_tensor(f"in_{k}", v.shape, F32, kind="ExternalInput").ap() for k, v in arrays.items()]
    out = nc.dram_tensor("block_out", (B, T, D), F32, kind="ExternalOutput").ap()
    block_kernel(nc, *args, out)
    r = run_bass_kernel_spmd(nc, [{f"in_{k}": v for k, v in arrays.items()}], core_ids=[0])
    return r.results[0]["block_out"]
```
